# Optimizing a Trainium2 kernel written in Bass

```python
import numpy as np
import jax
import jax.numpy as jnp

def _softmax(x, axis=-1):
    return jax.nn.softmax(x, axis=axis)

def _gelu(x):
    return jax.nn.gelu(x, approximate=True)

def _silu(x):
    return jax.nn.silu(x)

def _sigmoid(x):
    return jax.nn.sigmoid(x)

def _layernorm(x, axis=-1, eps=1e-05):
    m = jnp.mean(x, axis=axis, keepdims=True)
    v = jnp.var(x, axis=axis, keepdims=True)
    return (x - m) / jnp.sqrt(v + eps)

def _scatter_add(tgt, idx, src, axis=0):
    return tgt.at[idx].add(src)

def _segment_sum(src, seg, n):
    return jax.ops.segment_sum(src, seg, n)
kernel_name = 'mk_adj_resnorm_d2_adj_r2_7fdf89'

def setup_inputs(seed: int=0):
    np.random.seed(seed)
    _w = jnp.asarray

    def _rec_inputs():
        import jax
        import jax.numpy as jnp
        _gk = jax.random.key(seed)
        x = -0.0004039 + 1 * jax.random.normal(jax.random.fold_in(_gk, 1), (128, 128, 384), jnp.float32)
        _a = jax.random.bernoulli(jax.random.fold_in(_gk, 2), 0.0625, (128, 128, 128))
        _af = _a.astype(jnp.float32)
        adj = _af
        return (x, adj)
    x, adj = _rec_inputs()

    def _L0_gnn_setup():
        import jax, jax.numpy as jnp
        import numpy as np
        B, S, H, L = (32, 256, 384, 2)

        def _layer_norm(z, a, b, eps=0.001):
            mu = jnp.mean(z, axis=-1, keepdims=True)
            sigma = jnp.std(z, axis=-1, keepdims=True, ddof=1)
            return (z - mu) / (sigma + eps) * a + b
        key = jax.random.key(seed)
        ks = jax.random.split(key, 6)
        hidden_state = jax.random.normal(ks[0], (B, S, H), dtype=jnp.float32)
        adjacency_matrix = (jax.random.uniform(ks[1], (B, S, S)) < 0.2).astype(jnp.float32)
        W_left = 0.05 * jax.random.normal(ks[2], (L, H, H), dtype=jnp.float32)
        W_right = 0.05 * jax.random.normal(ks[3], (L, H, H), dtype=jnp.float32)
        W_lin = 0.05 * jax.random.normal(ks[4], (L, H, H), dtype=jnp.float32)
        b_lin = jnp.zeros((L, H), dtype=jnp.float32)
        ln_a = jnp.ones((L, H), dtype=jnp.float32)
        ln_b = jnp.zeros((L, H), dtype=jnp.float32)
        return {'hidden_state': hidden_state, 'adjacency_matrix': adjacency_matrix, 'W_left': W_left, 'W_right': W_right, 'W_lin': W_lin, 'b_lin': b_lin, 'ln_a': ln_a, 'ln_b': ln_b}
    _L0_gnn_all = _L0_gnn_setup()
    _L0_gnn_in = {k: v for k, v in _L0_gnn_all.items() if k in ('W_left', 'W_right', 'W_lin', 'b_lin', 'ln_a', 'ln_b')}
    del _L0_gnn_all

    def _L1_gnn_setup():
        import jax, jax.numpy as jnp
        import numpy as np
        NUM_HEADS = 12
        HIDDEN = 384
        HEAD = HIDDEN // NUM_HEADS
        B, N = (16, 256)
        key = jax.random.key(seed)
        ks = jax.random.split(key, 9)
        s = 0.02
        return {'x': jax.random.normal(ks[0], (B, N, HIDDEN), jnp.float32), 'spatial_encoding': jax.random.normal(ks[1], (B, N, N), jnp.float32), 'edge_encoding': jax.random.normal(ks[2], (B, N, N), jnp.float32), 'Wq': jax.random.normal(ks[3], (HIDDEN, HIDDEN), jnp.float32) * s, 'Wk': jax.random.normal(ks[4], (HIDDEN, HIDDEN), jnp.float32) * s, 'Wv': jax.random.normal(ks[5], (HIDDEN, HIDDEN), jnp.float32) * s, 'bv': jax.random.normal(ks[6], (HIDDEN,), jnp.float32) * s, 'Wo': jax.random.normal(ks[7], (HIDDEN, HIDDEN), jnp.float32) * s, 'bo': jax.random.normal(ks[8], (HIDDEN,), jnp.float32) * s}
    _L1_gnn_all = _L1_gnn_setup()
    _L1_gnn_in = {k: v for k, v in _L1_gnn_all.items() if k in ('Wq', 'Wk', 'Wv', 'bv', 'Wo', 'bo')}
    del _L1_gnn_all
    return {'x': x, 'adj': adj, 'L0_gnn_W_left': _L0_gnn_in['W_left'], 'L0_gnn_W_right': _L0_gnn_in['W_right'], 'L0_gnn_W_lin': _L0_gnn_in['W_lin'], 'L0_gnn_b_lin': _L0_gnn_in['b_lin'], 'L0_gnn_ln_a': _L0_gnn_in['ln_a'], 'L0_gnn_ln_b': _L0_gnn_in['ln_b'], 'L1_gnn_Wq': _L1_gnn_in['Wq'], 'L1_gnn_Wk': _L1_gnn_in['Wk'], 'L1_gnn_Wv': _L1_gnn_in['Wv'], 'L1_gnn_bv': _L1_gnn_in['bv'], 'L1_gnn_Wo': _L1_gnn_in['Wo'], 'L1_gnn_bo': _L1_gnn_in['bo']}

def reference(x, adj, L0_gnn_W_left, L0_gnn_W_right, L0_gnn_W_lin, L0_gnn_b_lin, L0_gnn_ln_a, L0_gnn_ln_b, L1_gnn_Wq, L1_gnn_Wk, L1_gnn_Wv, L1_gnn_bv, L1_gnn_Wo, L1_gnn_bo):
    import jax
    import jax.numpy as jnp

    def _L0_gnn_ref(hidden_state, adjacency_matrix, W_left, W_right, W_lin, b_lin, ln_a, ln_b):
        import jax, jax.numpy as jnp
        import numpy as np
        B, S, H, L = (32, 256, 384, 2)

        def _layer_norm(z, a, b, eps=0.001):
            mu = jnp.mean(z, axis=-1, keepdims=True)
            sigma = jnp.std(z, axis=-1, keepdims=True, ddof=1)
            return (z - mu) / (sigma + eps) * a + b
        temper = float(np.sqrt(H))
        adj = adjacency_matrix
        adj_tri = jnp.triu(adj, k=1)
        diag_mask = jnp.triu(adj, k=0) - adj_tri
        h = hidden_state
        for l in range(L):
            m_left = jnp.einsum('bsh,oh->bso', h, W_left[l])
            m_right = jnp.einsum('bsh,oh->bso', h, W_right[l])
            u_left = jnp.einsum('bih,bjh->bij', h, m_left) / temper
            u_right = jnp.einsum('bih,bjh->bij', h, m_right) / temper
            u = u_left * adj_tri + u_left * diag_mask + u_right * jnp.swapaxes(adj_tri, 1, 2)
            delta_exp_u = jnp.exp(u) * adj
            attention = delta_exp_u / (jnp.sum(delta_exp_u, axis=2, keepdims=True) + 1e-10)
            h_lin = jnp.einsum('bsh,oh->bso', h, W_lin[l]) + b_lin[l]
            ctx = jnp.matmul(attention, h_lin)
            h = jax.nn.relu(_layer_norm(ctx, ln_a[l], ln_b[l]))
        return h

    def _L1_gnn_ref(x, spatial_encoding, edge_encoding, Wq, Wk, Wv, bv, Wo, bo):
        import jax, jax.numpy as jnp
        import numpy as np
        NUM_HEADS = 12
        HIDDEN = 384
        HEAD = HIDDEN // NUM_HEADS
        B, N = (16, 256)
        b, n, h = x.shape
        scale = jnp.asarray(HIDDEN, x.dtype) ** (-0.5)
        q = (x @ Wq.T).reshape(b, n, NUM_HEADS, HEAD)
        k = (x @ Wk.T).reshape(b, n, NUM_HEADS, HEAD)
        v = (x @ Wv.T + bv).reshape(b, n, NUM_HEADS, HEAD)
        bias = (spatial_encoding + edge_encoding)[:, None]
        scores = jnp.einsum('bqhd,bkhd->bhqk', q, k) * scale + bias
        row_nonzero = jnp.any(scores != 0, axis=-1, keepdims=True)
        scores = jnp.where(row_nonzero, scores, -jnp.inf)
        p = jax.nn.softmax(scores, axis=-1)
        p = jnp.nan_to_num(p)
        out = jnp.einsum('bhqk,bkhd->bqhd', p, v).reshape(b, n, h)
        return out @ Wo.T + bo
    x = _layernorm(x + _L0_gnn_ref(x, adj, L0_gnn_W_left, L0_gnn_W_right, L0_gnn_W_lin, L0_gnn_b_lin, L0_gnn_ln_a, L0_gnn_ln_b), axis=-1)
    x = _layernorm(x + _L1_gnn_ref(x, adj, adj, L1_gnn_Wq, L1_gnn_Wk, L1_gnn_Wv, L1_gnn_bv, L1_gnn_Wo, L1_gnn_bo), axis=-1)
    return x

_drawn_inputs = setup_inputs


def setup_inputs(seed=0):
    import zlib

    import numpy as np

    out = dict(_drawn_inputs(seed))
    spreads = {'L0_gnn_b_lin': (0.0, 0.1), 'L0_gnn_ln_a': (1.0, 0.2), 'L0_gnn_ln_b': (0.0, 0.1)}
    factors = {'L1_gnn_Wq': 8.0, 'L1_gnn_Wk': 8.0, 'L1_gnn_bv': 6.292, 'L1_gnn_bo': 2.987}
    for name, (base, spread) in spreads.items():
        noise = np.random.default_rng([zlib.crc32(name.encode()), seed]).standard_normal(out[name].shape)
        drawn = base * np.exp(spread * noise) if base else spread * noise
        out[name] = jnp.asarray(drawn.astype(out[name].dtype))
    for name, factor in factors.items():
        out[name] = (out[name] * factor).astype(out[name].dtype)
    return out
```

```python
import concourse.bass as bass
from concourse import mybir
from contextlib import ExitStack

GRAPHS, TOK, FEAT = 128, 128, 384
GROUP = 4
GROUPS = GRAPHS // GROUP
KB = FEAT // 128
HEADS = 12
HEAD = FEAT // HEADS
TILES = 128 // HEAD
GT = GROUP * TOK
VCOL = HEAD + 1
HCOL = FEAT + 2
TEMPER = float(FEAT) ** 0.5
WSCALE = 64.0
BIG = 3.0e38


class Signal:

    def __init__(self, sem, per_group):
        self.sem, self.per_group = sem, per_group

    def upto(self, group, n):
        return group * self.per_group + n


def program(nc, x, adj, weights, biases, ln_cols, ln_rows, out):
    f32, f32r, f16 = mybir.dt.float32, mybir.dt.float32r, mybir.dt.float16
    i32 = mybir.dt.int32
    ALU, ACT, AX = mybir.AluOpType, mybir.ActivationFunctionType, mybir.AxisListType
    mm, transpose = nc.tensor.matmul, nc.tensor.transpose

    with ExitStack() as stack:
        def sb(name, shape, dt=f32):
            return stack.enter_context(nc.sbuf_tensor(name, [128] + shape, dt))

        def sem(name):
            return stack.enter_context(nc.semaphore(name))

        ident = sb("ident", [128])
        keep_left = sb("keep_left", [TOK])
        keep_right = sb("keep_right", [TOK])
        ones_r = sb("ones_r", [128], f32r)
        ones_h = sb("ones_h", [128], f16)
        pw = sb("pw", [2, GROUP])
        wr_hi, wr_lo = (sb(f"wr_{p}", [6, KB, FEAT], f32r) for p in ("hi", "lo"))
        wh_hi, wh_lo = (sb(f"wh_{p}", [4, KB, FEAT], f16) for p in ("hi", "lo"))
        bias_r = sb("bias_r", [2, FEAT], f32r)
        bias_h = sb("bias_h", [2, FEAT], f16)
        lncol = sb("lncol", [2, KB])
        lnrow = sb("lnrow", [2, FEAT])
        xin = sb("xin", [GROUP, FEAT])
        xres = sb("xres", [GROUP, FEAT])
        adjn = sb("adjn", [GROUP, TOK])
        adjT = sb("adjT", [GROUP, TOK])
        mask = sb("mask", [GROUP, 2, TOK])
        hT_hi, hT_lo = (sb(f"hT_{p}", [KB, GROUP, TOK], f32r) for p in ("hi", "lo"))
        nT_hi, nT_lo = (sb(f"nT_{p}", [KB, 2, GROUP, TOK], f32r) for p in ("hi", "lo"))
        hl_hi, hl_lo = (sb(f"hl_{p}", [GROUP, HCOL], f32r) for p in ("hi", "lo"))
        uLR = sb("uLR", [2, 2, TOK])
        e = sb("e", [GROUP, TOK])
        e_hi, e_lo = (sb(f"e_{p}", [GROUP, TOK], f32r) for p in ("hi", "lo"))
        z = sb("z", [GROUP, FEAT])
        hT = sb("hT", [2, GROUP, TOK])
        x1 = sb("x1", [GROUP, FEAT])
        eps_den, rden = sb("eps_den", [GROUP]), sb("rden", [GROUP])
        st, mv = sb("st", [GROUP, 6]), sb("mv", [GROUP, 2])
        var, rstd, nmr = sb("var", [GROUP]), sb("rstd", [GROUP]), sb("nmr", [GROUP])
        sd = sb("sd", [GROUP])
        adj2 = sb("adj2", [GROUP, TOK])
        xT_hi, xT_lo = (sb(f"xT_{p}", [KB, GROUP, TOK], f16) for p in ("hi", "lo"))
        qk_hi, qk_lo = (sb(f"qk_{p}", [2, KB, GROUP, TOK], f16) for p in ("hi", "lo"))
        v_hi, v_lo = (sb(f"v_{p}", [GROUP, HEADS, VCOL], f16) for p in ("hi", "lo"))
        s = sb("s", [HEADS, TOK])
        nmax, nmin, live = sb("nmax", [HEADS]), sb("nmin", [HEADS]), sb("live", [2, HEADS])
        pT_hi, pT_lo = (sb(f"pT_{p}", [HEADS, TOK], f16) for p in ("hi", "lo"))
        rs = sb("rs", [2, HEADS])
        o = sb("o", [HEADS, HEAD])
        oT_hi, oT_lo = (sb(f"oT_{p}", [KB, TOK], f16) for p in ("hi", "lo"))
        y2 = sb("y2", [2, FEAT])
        st2, mv2 = sb("st2", [6]), sb("mv2", [2])
        var2, rstd2, nmr2 = sb("var2", [1]), sb("rstd2", [1]), sb("nmr2", [1])

        psum = stack.enter_context(nc.psum_tensor("psum", [128, 8, 512], f32))
        PJ, MX, SC = (0, 1), (2, 3), (4, 5, 6, 7)

        def signal(name, per_group):
            return Signal(sem(name), per_group)

        x_in, adj_in, xres_in = signal("x_in", 16), signal("adj_in", 16), signal("xres_in", 16)
        adj2_in = signal("adj2_in", 16)
        out_st = [signal(f"out_st{i}", 32) for i in range(2)]
        xt_full, xt_hi, xt_lo = (signal(f"xt_{p}", KB) for p in ("full", "hi", "lo"))
        adjT_full, adjT_ok, mask_ok = signal("adjT_full", 1), signal("adjT_ok", 1), signal("mask_ok", 2)
        nl_full, nl_hi, nl_lo = ([signal(f"nl{l}_{p}", 2 * KB) for l in range(2)] for p in ("full", "hi", "lo"))
        hl_full, hlr_hi, hlr_lo = ([signal(f"hl{l}_{p}", GROUP) for l in range(2)] for p in ("full", "hi", "lo"))
        u_full, u_read, u_sum, e_raw, e_ok, e_hi_ok, e_lo_ok = (
            [signal(f"{p}{l}", 2) for l in range(2)]
            for p in ("u_full", "u_read", "u_sum", "e_raw", "e_ok", "e_hi_ok", "e_lo_ok"))
        c_full, den_ok, rden_ok, z_ok, st_ok, mv_ok, n_ok = (
            [signal(f"{p}{l}", GROUP) for l in range(2)]
            for p in ("c_full", "den_ok", "rden_ok", "z_ok", "st_ok", "mv_ok", "n_ok"))
        var_ok, pow_ok, eps_ok, rstd_ok, nmr_ok = (
            [signal(f"{p}{l}", 1) for l in range(2)] for p in ("var_ok", "pow_ok", "eps_ok", "rstd_ok", "nmr_ok"))
        th_full, th_raw, th_hi, th_lo = (signal(f"th_{p}", KB) for p in ("full", "raw", "hi", "lo"))
        za_ok, zb_ok, y_ok, yst_ok, ymv_ok, x1_ok = (
            signal(p, GROUP) for p in ("za_ok", "zb_ok", "y_ok", "yst_ok", "ymv_ok", "x1_ok"))
        yvar_ok, ypow_ok, ynmr_ok = (signal(p, 1) for p in ("yvar_ok", "ypow_ok", "ynmr_ok"))
        x1t_full, x1t_hi, x1t_lo = (signal(f"x1t_{p}", KB) for p in ("full", "hi", "lo"))
        qk_full, qkr_hi, qkr_lo = (signal(f"qk_{p}", 2 * KB) for p in ("full", "hi", "lo"))
        v_full, vr_hi, vr_lo = (signal(f"v_{p}", GROUP) for p in ("full", "hi", "lo"))
        adj2_ok = signal("adj2_ok", 1)
        s_full, s_ok, s_min, p_ok = (signal(p, GROUP * TILES) for p in ("s_full", "s_ok", "s_min", "p_ok"))
        pt_full, pt_hi, pt_lo = (signal(f"pt_{p}", GROUP * KB) for p in ("full", "hi", "lo"))
        pv_full, live1, live2, rs1, rs2, o_ok = (
            signal(p, GROUP) for p in ("pv_full", "live1", "live2", "rs1", "rs2", "o_ok"))
        to_full, to_hi, to_lo = (signal(f"to_{p}", GROUP) for p in ("full", "hi", "lo"))
        po_full, y2_ok, y2st_ok, y2mv_ok, y2var_ok, y2pow_ok, y2nmr_ok, fin_ok = (
            signal(p, GROUP) for p in ("po_full", "y2_ok", "y2st_ok", "y2mv_ok", "y2var_ok", "y2pow_ok",
                                       "y2nmr_ok", "fin_ok"))
        ld, w_hi_ok, w_lo_ok, const_ok, ones_ok, b_ok, b_lo = (
            sem(p) for p in ("ld", "w_hi_ok", "w_lo_ok", "const_ok", "ones_ok", "b_ok", "b_lo"))
        w_in = [sem(f"w_in{i}") for i in range(2)]

        ADVANCED = (adj2_in, *out_st, x1t_full, x1t_hi, x1t_lo, qk_full, qkr_hi, qkr_lo, v_full, vr_hi, vr_lo,
                    adj2_ok, s_full, s_ok, s_min, p_ok, pt_full, pt_hi, pt_lo, pv_full, live1, live2, rs1, rs2,
                    o_ok, to_full, to_hi, to_lo, po_full, y2_ok, y2st_ok, y2mv_ok, y2var_ok, y2pow_ok,
                    y2nmr_ok, fin_ok)

        def uses(name, n, read):
            return [(name, i, read) for i in range(n)]

        PJ_ORDER = (uses("nl0", 2 * KB, nl_lo[0]) + uses("qk", 2 * KB, qkr_lo) + uses("v", GROUP, vr_lo)
                    + uses("hl0", GROUP, hlr_lo[0]) + [("po", 0, y2_ok), ("po", 1, y2_ok)]
                    + uses("nl1", 2 * KB, nl_lo[1]) + uses("hl1", GROUP, hlr_lo[1])
                    + [("po", 2, y2_ok), ("po", 3, y2_ok)])
        MX_ORDER = (uses("x1t", KB, x1t_lo) + uses("u0", 2, u_read[0]) + [("pv", 0, o_ok)]
                    + uses("c0", GROUP, z_ok[0]) + [("to", 0, to_lo), ("pv", 1, o_ok)] + uses("th", KB, th_hi)
                    + [("to", 1, to_lo), ("pv", 2, o_ok)] + uses("u1", 2, u_read[1])
                    + [("to", 2, to_lo), ("pv", 3, o_ok)] + uses("xt", KB, xt_lo) + [("adjT", 0, adjT_ok)]
                    + uses("c1", GROUP, z_ok[1]) + [("to", 3, to_lo)])
        L1_STAGES = ("x1t", "qk", "v", "pv", "to", "po")
        NEXT_STAGES = ("xt", "adjT")

        def place(stage, i):
            for order, banks in ((PJ_ORDER, PJ), (MX_ORDER, MX)):
                for n, use in enumerate(order):
                    if use[:2] == (stage, i):
                        return order, n, banks[n % 2]

        def bank(stage, i):
            return psum[:, place(stage, i)[2], :]

        class Pass:

            def __init__(self, it, l0=True, l1=True, nxt=True, first=False):
                self.it, self.l0, self.l1, self.nxt, self.first = it, l0, l1, nxt, first

            def has(self, stage):
                return self.l1 if stage in L1_STAGES else self.nxt if stage in NEXT_STAGES else self.l0

            def group(self, signal_or_stage):
                return self.it + 1 if signal_or_stage in (xt_full, xt_hi, xt_lo, adjT_full, adjT_ok) else self.it

            def await_(self, eng, sig, n):
                eng.wait_ge(sig.sem, sig.upto(self.group(sig), n))

            def await_apart(self, eng, sig, n):
                value = sig.upto(self.group(sig), n)
                if not isinstance(value, int):
                    value = eng.snap(eng.to_reg(value), min_val=1)
                eng.wait_ge(sig.sem, 1)
                eng.wait_ge(sig.sem, value)

            def await_prev(self, eng, sig, n):
                if not self.first:
                    eng.wait_ge(sig.sem, sig.upto(self.group(sig) - 1, n))

            def await_bank(self, eng, stage, i):
                order, n, _ = place(stage, i)
                for m in range(n - 2, -1, -2):
                    name, j, read = order[m]
                    if self.has(name):
                        self.await_(eng, read, j + 1)
                        return
                last = max(m for m in range(len(order)) if m % 2 == n % 2)
                name, j, read = order[last]
                self.await_prev(eng, read, j + 1)

        def passes(eng, body, head=None):
            if head:
                head()
            body(Pass(0, l1=False, first=True))
            with eng.Fori(1, GROUPS - 1) as it:
                body(Pass(it))
            body(Pass(GROUPS - 1, nxt=False))
            body(Pass(GROUPS, l0=False, nxt=False))

        stage_w = [z[:, 0:KB], x1[:, 0:KB]]
        stage_b = s[:].rearrange("p (a h) t -> p a (h t)", a=4)

        block = stack.enter_context(nc.Block())

        @block.sync
        def _(sp):
            for m in range(10):
                if m >= 2:
                    sp.wait_ge(w_lo_ok, m - 1)
                sp.dma_start(stage_w[m % 2], weights[m]).then_inc(w_in[m % 2], 16)
                if m == 1:
                    sp.dma_start(xin[:], x[0:GROUP].rearrange("b t f -> t b f")).then_inc(x_in.sem, 16)
                    sp.dma_start(adjn[:], adj[0:GROUP].rearrange("b i j -> i b j")).then_inc(adj_in.sem, 16)
            sp.dma_start(lncol[:], ln_cols).then_inc(ld, 16)
            sp.dma_start(lnrow[:], ln_rows.rearrange("a f -> (a f)")[None, :].to_broadcast([128, 2 * FEAT])).then_inc(ld, 16)
            sp.wait_ge(const_ok, 1)
            for half in range(2):
                sp.dma_start(stage_b[32 * half:32 * half + 1, :, :], biases[None, :, :]).then_inc(ld, 16)
            for sig in ADVANCED:
                sp.sem_inc(sig.sem, sig.per_group)

            def body(p):
                it = p.it
                if p.l1:
                    p.await_prev(sp, s_ok, GROUP * TILES)
                    sp.dma_start(adj2[:], adj[bass.ds((it - 1) * GROUP, GROUP)].rearrange("b i j -> i b j"))\
                        .then_inc(adj2_in.sem, 16)
                if p.nxt:
                    sp.wait_ge(xt_full.sem, xt_full.upto(it, KB))
                    sp.dma_start(xin[:], x[bass.ds((it + 1) * GROUP, GROUP)].rearrange("b t f -> t b f"))\
                        .then_inc(x_in.sem, 16)
                    sp.wait_ge(adjT_full.sem, adjT_full.upto(it, 1))
                    sp.wait_ge(mask_ok.sem, mask_ok.upto(it, 2))
                    sp.dma_start(adjn[:], adj[bass.ds((it + 1) * GROUP, GROUP)].rearrange("b i j -> i b j"))\
                        .then_inc(adj_in.sem, 16)
                if p.l0:
                    p.await_prev(sp, y_ok, GROUP)
                    sp.dma_start(xres[:], x[bass.ds(it * GROUP, GROUP)].rearrange("b t f -> t b f"))\
                        .then_inc(xres_in.sem, 16)
                if p.l1:
                    for b in range(GROUP):
                        p.await_(sp, fin_ok, b + 1)
                        sp.dma_start(out[bass.ds((it - 1) * GROUP + b, 1)].rearrange("b t f -> t (b f)"), y2[:, b % 2])\
                            .then_inc(out_st[b % 2].sem, 16)

            passes(sp, body)
            for i in range(2):
                sp.wait_ge(out_st[i].sem, out_st[i].upto(GROUPS, 32))

        @block.gpsimd
        def _(pool):
            nc.gpsimd.memset(stage_b[:], 0.0).then_inc(const_ok, 1)
            nc.gpsimd.memset(ident[:], 0.0).then_inc(b_ok, 1)
            nc.gpsimd.memset(keep_left[:], 1.0 / TEMPER).then_inc(b_ok, 1)
            nc.gpsimd.memset(keep_right[:], 1.0 / TEMPER).then_inc(b_ok, 1)
            nc.gpsimd.memset(pw[:, 0], 0.5).then_inc(ones_ok, 1)
            nc.gpsimd.memset(pw[:, 1], -0.5).then_inc(ones_ok, 1)
            nc.gpsimd.memset(ones_r[:].bitcast(f32), 1.0).then_inc(ones_ok, 1)
            nc.gpsimd.memset(ones_h[:], 1.0).then_inc(ones_ok, 1)
            nc.gpsimd.memset(hl_hi[:, :, FEAT:FEAT + 1].bitcast(f32), 1.0).then_inc(ones_ok, 1)
            nc.gpsimd.memset(hl_hi[:, :, FEAT + 1:HCOL].bitcast(f32), 0.0).then_inc(ones_ok, 1)
            nc.gpsimd.memset(hl_lo[:, :, FEAT:HCOL].bitcast(f32), 0.0).then_inc(ones_ok, 1)
            nc.gpsimd.memset(v_hi[:, :, :, HEAD:VCOL], 1.0).then_inc(ones_ok, 1)
            nc.gpsimd.memset(v_lo[:, :, :, HEAD:VCOL], 0.0).then_inc(ones_ok, 1)
            pool.wait_ge(b_ok, 3)
            nc.gpsimd.affine_select(out=ident[:], in_=ident[:], compare_op=ALU.not_equal, fill=1.0, base=0,
                                    pattern=[[-1, 128]], channel_multiplier=1).then_inc(const_ok, 1)
            nc.gpsimd.affine_select(out=keep_left[:], in_=keep_left[:], compare_op=ALU.is_ge, fill=0.0, base=0,
                                    pattern=[[-1, TOK]], channel_multiplier=1).then_inc(const_ok, 1)
            nc.gpsimd.affine_select(out=keep_right[:], in_=keep_right[:], compare_op=ALU.is_gt, fill=0.0, base=0,
                                    pattern=[[1, TOK]], channel_multiplier=-1).then_inc(const_ok, 1)
            pool.wait_ge(const_ok, 4)
            pool.wait_ge(ones_ok, 9)

            def masks(p, sig_group):
                pool.wait_ge(adj_in.sem, adj_in.upto(sig_group, 16))
                pool.wait_ge(adjT_ok.sem, adjT_ok.upto(sig_group, 1))
                if p is not None:
                    p.await_(pool, u_read[1], 2)
                nc.gpsimd.tensor_tensor(mask[:, :, 0], adjT[:], keep_L, ALU.mult).then_inc(mask_ok.sem, 1)
                nc.gpsimd.tensor_tensor(mask[:, :, 1], adjn[:], keep_R, ALU.mult).then_inc(mask_ok.sem, 1)

            keep_L = keep_left[:, None, :].to_broadcast([128, GROUP, TOK])
            keep_R = keep_right[:, None, :].to_broadcast([128, GROUP, TOK])

            def weigh(p, l):
                for h in range(2):
                    part = slice(2 * h, 2 * h + 2)
                    p.await_(pool, e_raw[l], h + 1)
                    nc.gpsimd.tensor_tensor(e[:, part], e[:, part], adjT[:, part], ALU.mult).then_inc(e_ok[l].sem, 1)
                for h in range(2):
                    part = slice(2 * h, 2 * h + 2)
                    p.await_(pool, e_hi_ok[l], h + 1)
                    p.await_(pool, e_ok[l], h + 1)
                    nc.gpsimd.tensor_tensor(e_lo[:, part], e[:, part], e_hi[:, part].bitcast(f32), ALU.subtract)\
                        .then_inc(e_lo_ok[l].sem, 1)

            def power(p, src_ok, dst, src, exponent, done, n=1):
                p.await_(pool, src_ok, n)
                w = dst.shape[-1]
                nc.gpsimd.tensor_tensor(dst, src, pw[:, exponent, 0:w], ALU.pow).then_inc(done.sem, 1)

            def body(p):
                if p.l1:
                    p.await_apart(pool, adj2_in, 16)
                    nc.gpsimd.tensor_scalar(adj2[:], adj2[:], 2.0, TEMPER, ALU.mult, ALU.mult)\
                        .then_inc(adj2_ok.sem, 1)
                if p.l0:
                    weigh(p, 0)
                    power(p, var_ok[0], sd[:], var[:], 0, pow_ok[0])
                if p.l1:
                    power(p, y2var_ok, rstd2[:], var2[:], 1, y2pow_ok, 1)
                    power(p, y2var_ok, rstd2[:], var2[:], 1, y2pow_ok, 2)
                if p.l0:
                    weigh(p, 1)
                if p.l1:
                    power(p, y2var_ok, rstd2[:], var2[:], 1, y2pow_ok, 3)
                if p.nxt:
                    masks(p, p.it + 1)
                if p.l0:
                    power(p, var_ok[1], sd[:], var[:], 0, pow_ok[1])
                if p.l1:
                    power(p, y2var_ok, rstd2[:], var2[:], 1, y2pow_ok, 4)
                if p.l0:
                    for b in range(GROUP):
                        p.await_(pool, n_ok[1], b + 1)
                        nc.gpsimd.tensor_tensor(z[:, b], z[:, b], lnrow[:, 0], ALU.mult).then_inc(za_ok.sem, 1)
                        p.await_(pool, za_ok, b + 1)
                        nc.gpsimd.tensor_tensor(z[:, b], z[:, b], lnrow[:, 1], ALU.add).then_inc(zb_ok.sem, 1)
                    power(p, yvar_ok, sd[:], var[:], 1, ypow_ok)

            def head():
                pool.wait_ge(ld, 64)
                masks(None, 0)

            passes(pool, body, head)

        @block.scalar
        def _(act):
            def copy(dst, src, scale=1.0):
                return nc.scalar.activation(dst, src, ACT.Copy, scale=scale)

            def hi(p, full, n, stage, dst, done, scale=1.0):
                p.await_(act, full, n + 1)
                w = 1
                for d in dst.shape[1:]:
                    w *= d
                src = bank(stage, n)[:, 0:w]
                if len(dst.shape) == 3:
                    src = src.rearrange("p (a b) -> p a b", a=dst.shape[1])
                copy(dst, src, scale).then_inc(done.sem, 1)

            def xt(p):
                for k in range(KB):
                    hi(p, xt_full, k, "xt", hT_hi[:, k], xt_hi)
                p.await_(act, adjT_full, 1)
                if not p.first:
                    act.wait_ge(e_ok[1].sem, e_ok[1].upto(p.it, 2))
                copy(adjT[:], bank("adjT", 0).rearrange("p (a b) -> p a b", a=GROUP)).then_inc(adjT_ok.sem, 1)

            def nl(p, l):
                for c in range(2 * KB):
                    lr, kb = divmod(c, KB)
                    hi(p, nl_full[l], c, f"nl{l}", nT_hi[:, kb, lr], nl_hi[l])

            def hl(p, l, b):
                hi(p, hl_full[l], b, f"hl{l}", hl_hi[:, b, 0:FEAT], hlr_hi[l])

            def exps(p, b, j):
                p.await_(act, s_min, b * TILES + j + 1)
                for c in range(KB):
                    h = TILES * c + j
                    last = nc.scalar.activation(s[:, h], s[:, h], ACT.Exp, bias=nmax[:, h:h + 1], scale=-1.0)
                last.then_inc(p_ok.sem, 1)

            def exp_u(p, l):
                for h in range(2):
                    p.await_(act, u_sum[l], h + 1)
                    nc.scalar.activation(e[:, 2 * h:2 * h + 2], e[:, 2 * h:2 * h + 2], ACT.Exp).then_inc(e_raw[l].sem, 1)
                for h in range(2):
                    p.await_(act, e_ok[l], h + 1)
                    copy(e_hi[:, 2 * h:2 * h + 2], e[:, 2 * h:2 * h + 2]).then_inc(e_hi_ok[l].sem, 1)

            def pt(p, b):
                for c in range(KB):
                    p.await_(act, pt_full, b * KB + c + 1)
                    copy(pT_hi[:, TILES * c:TILES * (c + 1)],
                         psum[:, SC[c], :].rearrange("p (a b) -> p a b", a=TILES)).then_inc(pt_hi.sem, 1)

            def ctx(p, l):
                for b in range(GROUP):
                    p.await_(act, rden_ok[l], b + 1)
                    copy(z[:, b], bank(f"c{l}", b)[:, 0:FEAT], scale=rden[:, b:b + 1]).then_inc(z_ok[l].sem, 1)

            def th(p):
                for k in range(KB):
                    p.await_(act, th_full, k + 1)
                    src = bank("th", k).rearrange("p (a b) -> p a b", a=GROUP)
                    if k == 2:
                        p.await_(act, th_lo, 1)
                    for dst, done in ((hT[:, k % 2], th_raw), (hT_hi[:, k], th_hi)):
                        nc.scalar.activation(dst, src, ACT.Relu, bias=lncol[:, 1, k:k + 1], scale=lncol[:, 0, k:k + 1])\
                            .then_inc(done.sem, 1)

            def to(p, b):
                hi(p, to_full, b, "to", oT_hi[:], to_hi)

            def body(p):
                if p.l0:
                    nl(p, 0)
                if p.l1:
                    for k in range(KB):
                        hi(p, x1t_full, k, "x1t", xT_hi[:, k], x1t_hi)
                    for c in range(2 * KB):
                        hi(p, qk_full, c, "qk", qk_hi[:, c // KB, c % KB], qkr_hi, 1.0 / WSCALE)
                    for b in range(GROUP):
                        p.await_(act, v_full, b + 1)
                        copy(v_hi[:, b, :, 0:HEAD], bank("v", b)[:, 0:FEAT].rearrange("p (h d) -> p h d", h=HEADS),
                             1.0 / WSCALE).then_inc(vr_hi.sem, 1)
                for j in range(TILES):
                    if p.l0:
                        hl(p, 0, j)
                    if p.l1:
                        exps(p, 0, j)
                if p.l0:
                    exp_u(p, 0)
                if p.l1:
                    pt(p, 0)
                if p.l0:
                    ctx(p, 0)
                if p.l1:
                    to(p, 0)
                    for j in range(TILES):
                        exps(p, 1, j)
                    pt(p, 1)
                if p.l0:
                    th(p)
                if p.l1:
                    to(p, 1)
                    for j in range(TILES):
                        exps(p, 2, j)
                if p.l0:
                    nl(p, 1)
                if p.l1:
                    pt(p, 2)
                for j in range(TILES):
                    if p.l0:
                        hl(p, 1, j)
                    if p.l1:
                        exps(p, 3, j)
                if p.l0:
                    exp_u(p, 1)
                if p.l1:
                    to(p, 2)
                    pt(p, 3)
                if p.nxt:
                    xt(p)
                if p.l0:
                    ctx(p, 1)
                if p.l1:
                    to(p, 3)

            def head():
                for m in range(10):
                    act.wait_ge(w_in[m % 2], 16 * (m // 2 + 1))
                    if m < 6:
                        copy(wr_hi[:, m], stage_w[m % 2]).then_inc(w_hi_ok, 1)
                    else:
                        copy(wh_hi[:, m - 6], stage_w[m % 2], WSCALE).then_inc(w_hi_ok, 1)
                xt(Pass(-1, l0=False, l1=False, first=True))

            passes(act, body, head)

        @block.vector
        def _(dve):
            def lo(p, hi_ok, n, stage, dst, rounded, done, scale=None):
                p.await_(dve, hi_ok, n + 1)
                w = 1
                for d in dst.shape[1:]:
                    w *= d
                src = bank(stage, n)[:, 0:w]
                if len(dst.shape) == 3:
                    src = src.rearrange("p (a b) -> p a b", a=dst.shape[1])
                if scale is None:
                    nc.vector.tensor_tensor(dst, src, rounded, ALU.subtract).then_inc(done.sem, 1)
                else:
                    nc.vector.scalar_tensor_tensor(dst, src, scale, rounded, ALU.mult, ALU.subtract)\
                        .then_inc(done.sem, 1)

            def xt(p):
                for k in range(KB):
                    lo(p, xt_hi, k, "xt", hT_lo[:, k], hT_hi[:, k].bitcast(f32), xt_lo)

            def nl(p, l, cs):
                for c in cs:
                    lr, kb = divmod(c, KB)
                    lo(p, nl_hi[l], c, f"nl{l}", nT_lo[:, kb, lr], nT_hi[:, kb, lr].bitcast(f32), nl_lo[l])

            def hl(p, l, b):
                lo(p, hlr_hi[l], b, f"hl{l}", hl_lo[:, b, 0:FEAT], hl_hi[:, b, 0:FEAT].bitcast(f32), hlr_lo[l])

            def scores(p, b, j):
                if b == 0 and j == 0:
                    p.await_apart(dve, adj2_ok, 1)
                p.await_apart(dve, s_full, b * TILES + j + 1)
                for c in range(KB):
                    h = TILES * c + j
                    last = nc.vector.tensor_tensor_reduce(
                        out=s[:, h], in0=psum[:, SC[j], c * TOK:(c + 1) * TOK], in1=adj2[:, b],
                        scale=-1.0 / TEMPER, scalar=BIG, op0=ALU.add, op1=ALU.min, accum_out=nmax[:, h:h + 1])
                last.then_inc(s_ok.sem, 1)
                p.await_(dve, s_ok, b * TILES + j + 1)
                nc.vector.tensor_reduce(nmin[:, j::TILES], s[:, j::TILES], AX.X, ALU.max).then_inc(s_min.sem, 1)

            def guard(p, b):
                p.await_(dve, s_min, (b + 1) * TILES)
                nc.vector.tensor_scalar(live[:, 0], nmax[:], 0.0, None, ALU.not_equal).then_inc(live1.sem, 1)
                p.await_(dve, live1, b + 1)
                nc.vector.scalar_tensor_tensor(live[:, 1], nmin[:], 0.0, live[:, 0], ALU.not_equal, ALU.max)\
                    .then_inc(live2.sem, 1)

            def pt(p, b):
                for c in range(KB):
                    p.await_(dve, pt_hi, b * KB + c + 1)
                    hs = slice(TILES * c, TILES * (c + 1))
                    nc.vector.tensor_tensor(pT_lo[:, hs], psum[:, SC[c], :].rearrange("p (a b) -> p a b", a=TILES),
                                            pT_hi[:, hs], ALU.subtract).then_inc(pt_lo.sem, 1)

            def pv(p, b):
                src = bank("pv", b)[:, 0:HEADS * VCOL].rearrange("p (h d) -> p h d", h=HEADS)
                p.await_(dve, pv_full, b + 1)
                nc.vector.reciprocal(rs[:, 0], src[:, :, HEAD]).then_inc(rs1.sem, 1)
                p.await_(dve, rs1, b + 1)
                p.await_(dve, live2, b + 1)
                nc.vector.tensor_tensor(rs[:, 1], rs[:, 0], live[:, 1], ALU.mult).then_inc(rs2.sem, 1)
                p.await_(dve, rs2, b + 1)
                nc.vector.tensor_tensor(o[:], src[:, :, 0:HEAD],
                                        rs[:, 1, :, None].to_broadcast([128, HEADS, HEAD]), ALU.mult)\
                    .then_inc(o_ok.sem, 1)

            def to(p, b):
                lo(p, to_hi, b, "to", oT_lo[:], oT_hi[:], to_lo)

            def po(p, b):
                p.await_(dve, po_full, b + 1)
                if b >= 2:
                    p.await_(dve, out_st[b % 2], 16)
                else:
                    p.await_prev(dve, out_st[b % 2], 32)
                nc.vector.scalar_tensor_tensor(y2[:, b % 2], bank("po", b)[:, 0:FEAT], 1.0 / WSCALE, x1[:, b],
                                               ALU.mult, ALU.add).then_inc(y2_ok.sem, 1)
                p.await_(dve, y2_ok, b + 1)
                nc.vector.bn_stats(st2[:], y2[:, b % 2]).then_inc(y2st_ok.sem, 1)
                p.await_apart(dve, y2st_ok, b + 1)
                nc.vector.bn_aggr(mv2[:], st2[:]).then_inc(y2mv_ok.sem, 1)
                p.await_(dve, y2mv_ok, b + 1)
                nc.vector.tensor_scalar(var2[:], mv2[:, 1:2], 1e-5, None, ALU.add).then_inc(y2var_ok.sem, 1)

            def fin(p, b):
                p.await_(dve, y2pow_ok, b + 1)
                nc.vector.scalar_tensor_tensor(nmr2[:], mv2[:, 0:1], -1.0, rstd2[:], ALU.mult, ALU.mult)\
                    .then_inc(y2nmr_ok.sem, 1)
                p.await_(dve, y2nmr_ok, b + 1)
                nc.vector.tensor_scalar(y2[:, b % 2], y2[:, b % 2], rstd2[:], nmr2[:], ALU.mult, ALU.add)\
                    .then_inc(fin_ok.sem, 1)

            def u(p, l, h):
                p.await_(dve, u_full[l], h + 1)
                if h == 1:
                    p.await_(dve, u_sum[l], 1)
                if l == 0 and h == 0:
                    dve.wait_ge(mask_ok.sem, mask_ok.upto(p.it, 2))
                nc.vector.tensor_tensor(uLR[:], bank(f"u{l}", h).rearrange("p (b r t) -> p b r t", b=2, r=2),
                                        mask[:, 2 * h:2 * h + 2], ALU.mult).then_inc(u_read[l].sem, 1)
                p.await_(dve, u_read[l], h + 1)
                nc.vector.tensor_tensor(e[:, 2 * h:2 * h + 2], uLR[:, :, 0], uLR[:, :, 1], ALU.add)\
                    .then_inc(u_sum[l].sem, 1)

            def den(p, l, b):
                p.await_(dve, c_full[l], b + 1)
                nc.vector.tensor_scalar(eps_den[:, b:b + 1], bank(f"c{l}", b)[:, FEAT:FEAT + 1], 1e-10, None, ALU.add)\
                    .then_inc(den_ok[l].sem, 1)
                p.await_(dve, den_ok[l], b + 1)
                nc.vector.reciprocal(rden[:, b:b + 1], eps_den[:, b:b + 1]).then_inc(rden_ok[l].sem, 1)

            def stats(p, src, src_ok, st_done, mv_done, var_done, factor, eps):
                for b in range(GROUP):
                    p.await_(dve, src_ok, b + 1)
                    nc.vector.bn_stats(st[:, b], src[:, b]).then_inc(st_done.sem, 1)
                for b in range(GROUP):
                    p.await_apart(dve, st_done, b + 1)
                    nc.vector.bn_aggr(mv[:, b], st[:, b]).then_inc(mv_done.sem, 1)
                p.await_(dve, mv_done, GROUP)
                nc.vector.tensor_scalar(var[:], mv[:, :, 1], factor, eps, ALU.mult, ALU.add).then_inc(var_done.sem, 1)

            def norm(p, l):
                p.await_(dve, pow_ok[l], 1)
                nc.vector.tensor_scalar(var[:], sd[:], 1e-3, None, ALU.add).then_inc(eps_ok[l].sem, 1)
                p.await_(dve, eps_ok[l], 1)
                nc.vector.reciprocal(rstd[:], var[:]).then_inc(rstd_ok[l].sem, 1)
                p.await_(dve, rstd_ok[l], 1)
                nc.vector.scalar_tensor_tensor(nmr[:], mv[:, :, 0], -1.0, rstd[:], ALU.mult, ALU.mult)\
                    .then_inc(nmr_ok[l].sem, 1)
                p.await_(dve, nmr_ok[l], 1)
                for b in range(GROUP):
                    nc.vector.tensor_scalar(z[:, b], z[:, b], rstd[:, b:b + 1], nmr[:, b:b + 1], ALU.mult, ALU.add)\
                        .then_inc(n_ok[l].sem, 1)

            def th(p):
                for k in range(KB):
                    p.await_(dve, th_hi, k + 1)
                    nc.vector.tensor_tensor(hT_lo[:, k], hT[:, k % 2], hT_hi[:, k].bitcast(f32), ALU.subtract)\
                        .then_inc(th_lo.sem, 1)

            def resid(p):
                p.await_(dve, xres_in, 16)
                for b in range(GROUP):
                    p.await_(dve, zb_ok, b + 1)
                    nc.vector.scalar_tensor_tensor(x1[:, b], z[:, b], 0.0, xres[:, b], ALU.max, ALU.add)\
                        .then_inc(y_ok.sem, 1)
                stats(p, x1, y_ok, yst_ok, ymv_ok, yvar_ok, 1.0, 1e-5)

            def resid_norm(p):
                p.await_(dve, ypow_ok, 1)
                nc.vector.scalar_tensor_tensor(nmr[:], mv[:, :, 0], -1.0, sd[:], ALU.mult, ALU.mult)\
                    .then_inc(ynmr_ok.sem, 1)
                p.await_(dve, ynmr_ok, 1)
                for b in range(GROUP):
                    nc.vector.tensor_scalar(x1[:, b], x1[:, b], sd[:, b:b + 1], nmr[:, b:b + 1], ALU.mult, ALU.add)\
                        .then_inc(x1_ok.sem, 1)

            LSTAT = (FEAT / (FEAT - 1.0), 0.0)

            def body(p):
                if p.l0:
                    nl(p, 0, range(2 * KB))
                if p.l1:
                    for k in range(KB):
                        lo(p, x1t_hi, k, "x1t", xT_lo[:, k], xT_hi[:, k], x1t_lo)
                    for c in range(2 * KB):
                        lo(p, qkr_hi, c, "qk", qk_lo[:, c // KB, c % KB], qk_hi[:, c // KB, c % KB], qkr_lo, 1.0 / WSCALE)
                    for b in range(GROUP):
                        p.await_(dve, vr_hi, b + 1)
                        nc.vector.scalar_tensor_tensor(
                            v_lo[:, b, :, 0:HEAD], bank("v", b)[:, 0:FEAT].rearrange("p (h d) -> p h d", h=HEADS),
                            1.0 / WSCALE, v_hi[:, b, :, 0:HEAD], ALU.mult, ALU.subtract).then_inc(vr_lo.sem, 1)
                for j in range(TILES):
                    if p.l1:
                        scores(p, 0, j)
                    if p.l0:
                        hl(p, 0, j)
                if p.l1:
                    guard(p, 0)
                if p.l0:
                    u(p, 0, 0)
                    u(p, 0, 1)
                if p.l1:
                    pt(p, 0)
                    pv(p, 0)
                for j in range(TILES):
                    if p.l0:
                        den(p, 0, j)
                    if p.l1:
                        scores(p, 1, j)
                if p.l1:
                    guard(p, 1)
                    to(p, 0)
                if p.l0:
                    stats(p, z, z_ok[0], st_ok[0], mv_ok[0], var_ok[0], *LSTAT)
                if p.l1:
                    po(p, 0)
                if p.l0:
                    norm(p, 0)
                if p.l1:
                    fin(p, 0)
                    pt(p, 1)
                    pv(p, 1)
                if p.l0:
                    th(p)
                if p.l1:
                    to(p, 1)
                    scores(p, 2, 0)
                    scores(p, 2, 1)
                    po(p, 1)
                    scores(p, 2, 2)
                    scores(p, 2, 3)
                    guard(p, 2)
                    fin(p, 1)
                if p.l0:
                    nl(p, 1, range(2 * KB))
                if p.l1:
                    pt(p, 2)
                    pv(p, 2)
                for j in range(TILES):
                    if p.l1:
                        scores(p, 3, j)
                    if p.l0:
                        hl(p, 1, j)
                if p.l1:
                    guard(p, 3)
                if p.l0:
                    u(p, 1, 0)
                    u(p, 1, 1)
                if p.l1:
                    to(p, 2)
                    pt(p, 3)
                    po(p, 2)
                    pv(p, 3)
                    fin(p, 2)
                if p.nxt:
                    xt(p)
                if p.l0:
                    for b in range(GROUP):
                        den(p, 1, b)
                if p.l1:
                    to(p, 3)
                if p.l0:
                    stats(p, z, z_ok[1], st_ok[1], mv_ok[1], var_ok[1], *LSTAT)
                if p.l1:
                    po(p, 3)
                if p.l0:
                    norm(p, 1)
                if p.l1:
                    fin(p, 3)
                if p.l0:
                    resid(p)
                    resid_norm(p)

            def head():
                for m in range(10):
                    dve.wait_ge(w_hi_ok, m + 1)
                    if m < 6:
                        nc.vector.tensor_tensor(wr_lo[:, m], stage_w[m % 2], wr_hi[:, m].bitcast(f32), ALU.subtract)\
                            .then_inc(w_lo_ok, 1)
                    else:
                        nc.vector.scalar_tensor_tensor(wh_lo[:, m - 6], stage_w[m % 2], WSCALE, wh_hi[:, m - 6],
                                                       ALU.mult, ALU.subtract).then_inc(w_lo_ok, 1)
                dve.wait_ge(ld, 64)
                nc.vector.tensor_copy(bias_r[:], stage_b[:, 0:2]).then_inc(b_lo, 1)
                nc.vector.tensor_scalar(bias_h[:], stage_b[:, 2:4], WSCALE, None, ALU.mult).then_inc(b_lo, 1)
                dve.wait_ge(b_lo, 2)
                rows = slice(32, 64)
                nc.vector.tensor_tensor(stage_b[rows, 0:2], stage_b[rows, 0:2], bias_r[rows].bitcast(f32), ALU.subtract)\
                    .then_inc(b_lo, 1)
                nc.vector.scalar_tensor_tensor(stage_b[rows, 2:4], stage_b[rows, 2:4], WSCALE, bias_h[rows],
                                               ALU.mult, ALU.subtract).then_inc(b_lo, 1)
                dve.wait_ge(b_lo, 4)
                nc.vector.tensor_copy(bias_r[rows], stage_b[rows, 0:2]).then_inc(b_lo, 1)
                nc.vector.tensor_copy(bias_h[rows], stage_b[rows, 2:4]).then_inc(b_lo, 1)
                dve.wait_ge(b_lo, 6)
                xt(Pass(-1, l0=False, l1=False, first=True))

            passes(dve, body, head)

        @block.tensor
        def _(pe):
            def product(dst, terms, done, n=1):
                total = len(terms)
                for i, (a, b) in enumerate(terms):
                    last = mm(dst, a, b, start=(i == 0), stop=(i == total - 1))
                last.then_inc(done.sem, n)

            def split(a_hi, a_lo, b_hi, b_lo):
                return [(a_hi, b_hi), (a_hi, b_lo), (a_lo, b_hi)]

            def turn(stage, i, srcs, done):
                dst = bank(stage, i)
                for n, src in enumerate(srcs):
                    last = transpose(dst[:, n * 128:(n + 1) * 128], src, ident[:])
                last.then_inc(done.sem, 1)

            def xt(p):
                pe.wait_ge(x_in.sem, x_in.upto(p.it + 1, 16))
                for k in range(KB):
                    p.await_bank(pe, "xt", k)
                    turn("xt", k, [xin[:, b, k * 128:(k + 1) * 128] for b in range(GROUP)], xt_full)
                pe.wait_ge(adj_in.sem, adj_in.upto(p.it + 1, 16))
                p.await_bank(pe, "adjT", 0)
                turn("adjT", 0, [adjn[:, b] for b in range(GROUP)], adjT_full)

            def nl(p, l):
                for c in range(2 * KB):
                    lr, kb = divmod(c, KB)
                    p.await_bank(pe, f"nl{l}", c)
                    w = slice(kb * 128, (kb + 1) * 128)
                    product(bank(f"nl{l}", c), [t for k in range(KB) for t in split(
                        wr_hi[:, 3 * l + lr, k, w], wr_lo[:, 3 * l + lr, k, w],
                        hT_hi[:, k].rearrange("p b t -> p (b t)"), hT_lo[:, k].rearrange("p b t -> p (b t)"))],
                        nl_full[l])

            def hl(p, l):
                for b in range(GROUP):
                    p.await_bank(pe, f"hl{l}", b)
                    product(bank(f"hl{l}", b)[:, 0:FEAT], [t for k in range(KB) for t in split(
                        hT_hi[:, k, b], hT_lo[:, k, b], wr_hi[:, 3 * l + 2, k], wr_lo[:, 3 * l + 2, k])]
                        + [(ones_r[:], bias_r[:, l])], hl_full[l])

            def u(p, l):
                p.await_(pe, nl_lo[l], 2 * KB)
                for h in range(2):
                    p.await_bank(pe, f"u{l}", h)
                    for g in range(2):
                        b = 2 * h + g
                        dst = bank(f"u{l}", h)[:, g * 256:(g + 1) * 256].rearrange("p (r t) -> p r t", r=2)
                        terms = [t for k in range(KB) for t in split(
                            hT_hi[:, k, b], hT_lo[:, k, b], nT_hi[:, k, :, b], nT_lo[:, k, :, b])]
                        for i, (a, m) in enumerate(terms):
                            last = mm(dst, a, m, start=(i == 0), stop=(i == len(terms) - 1))
                    last.then_inc(u_full[l].sem, 1)

            def ctx(p, l):
                p.await_(pe, hlr_lo[l], GROUP)
                for b in range(GROUP):
                    if b % 2 == 0:
                        p.await_(pe, e_lo_ok[l], b // 2 + 1)
                    p.await_bank(pe, f"c{l}", b)
                    product(bank(f"c{l}", b)[:, 0:HCOL], split(e_hi[:, b], e_lo[:, b], hl_hi[:, b], hl_lo[:, b]),
                            c_full[l])

            def th(p):
                p.await_(pe, n_ok[0], GROUP)
                for k in range(KB):
                    p.await_bank(pe, "th", k)
                    turn("th", k, [z[:, b, k * 128:(k + 1) * 128] for b in range(GROUP)], th_full)

            def x1t(p):
                pe.wait_ge(x1_ok.sem, x1_ok.upto(p.it - 1, GROUP))
                for k in range(KB):
                    p.await_bank(pe, "x1t", k)
                    turn("x1t", k, [x1[:, b, k * 128:(k + 1) * 128] for b in range(GROUP)], x1t_full)

            def qk(p):
                p.await_(pe, x1t_lo, KB)
                for c in range(2 * KB):
                    p.await_bank(pe, "qk", c)
                    w = slice((c % KB) * 128, (c % KB + 1) * 128)
                    product(bank("qk", c), [t for k in range(KB) for t in split(
                        wh_hi[:, c // KB, k, w], wh_lo[:, c // KB, k, w],
                        xT_hi[:, k].rearrange("p b t -> p (b t)"), xT_lo[:, k].rearrange("p b t -> p (b t)"))],
                        qk_full)

            def v(p):
                for b in range(GROUP):
                    p.await_bank(pe, "v", b)
                    product(bank("v", b)[:, 0:FEAT], [t for k in range(KB) for t in split(
                        xT_hi[:, k, b], xT_lo[:, k, b], wh_hi[:, 2, k], wh_lo[:, 2, k])]
                        + [(ones_h[:], bias_h[:, 0])], v_full)

            def scores(p, b):
                if b == 0:
                    p.await_(pe, qkr_lo, 2 * KB)
                    p.await_prev(pe, pt_lo, GROUP * KB)
                else:
                    p.await_(pe, pt_lo, b * KB)
                    p.await_(pe, s_ok, b * TILES)
                for c in range(KB):
                    for i in range(3):
                        a, m = ((qk_hi, qk_hi), (qk_hi, qk_lo), (qk_lo, qk_hi))[i]
                        for j in range(TILES):
                            rows = slice(HEAD * j, HEAD * (j + 1))
                            last = mm(psum[:, SC[j], c * TOK:(c + 1) * TOK], a[rows, 0, c, b], m[rows, 1, c, b],
                                      start=(i == 0), stop=(i == 2))
                            if c == KB - 1 and i == 2:
                                last.then_inc(s_full.sem, 1)

            def pt(p, b):
                p.await_(pe, p_ok, (b + 1) * TILES)
                for c in range(KB):
                    for j in range(TILES):
                        last = transpose(psum[:, SC[c], j * TOK:(j + 1) * TOK], s[:, TILES * c + j], ident[:])
                    last.then_inc(pt_full.sem, 1)

            def pv(p, b):
                if b == 0:
                    p.await_(pe, vr_lo, GROUP)
                p.await_bank(pe, "pv", b)
                p.await_(pe, pt_lo, (b + 1) * KB)
                dst = bank("pv", b)
                for h in range(HEADS):
                    terms = split(pT_hi[:, h], pT_lo[:, h], v_hi[:, b, h], v_lo[:, b, h])
                    for i, (a, m) in enumerate(terms):
                        last = mm(dst[:, h * VCOL:(h + 1) * VCOL], a, m, start=(i == 0), stop=(i == 2))
                last.then_inc(pv_full.sem, 1)

            def to(p, b):
                p.await_(pe, o_ok, b + 1)
                p.await_bank(pe, "to", b)
                of = o[:].rearrange("p h d -> p (h d)")
                turn("to", b, [of[:, k * 128:(k + 1) * 128] for k in range(KB)], to_full)

            def po(p, b):
                p.await_(pe, to_lo, b + 1)
                p.await_bank(pe, "po", b)
                product(bank("po", b)[:, 0:FEAT], [t for k in range(KB) for t in split(
                    oT_hi[:, k], oT_lo[:, k], wh_hi[:, 3, k], wh_lo[:, 3, k])]
                    + [(ones_h[:], bias_h[:, 1])], po_full)

            def body(p):
                if p.l0:
                    pe.wait_ge(xt_lo.sem, xt_lo.upto(p.it, KB))
                    nl(p, 0)
                if p.l1:
                    x1t(p)
                    qk(p)
                    v(p)
                    scores(p, 0)
                if p.l0:
                    hl(p, 0)
                    u(p, 0)
                if p.l1:
                    pt(p, 0)
                    pv(p, 0)
                    scores(p, 1)
                if p.l0:
                    ctx(p, 0)
                if p.l1:
                    to(p, 0)
                    po(p, 0)
                    pt(p, 1)
                    pv(p, 1)
                    scores(p, 2)
                if p.l0:
                    th(p)
                if p.l1:
                    to(p, 1)
                    po(p, 1)
                if p.l0:
                    p.await_(pe, th_lo, KB)
                    nl(p, 1)
                if p.l1:
                    pt(p, 2)
                    pv(p, 2)
                    scores(p, 3)
                if p.l0:
                    hl(p, 1)
                    u(p, 1)
                if p.l1:
                    to(p, 2)
                    po(p, 2)
                    pt(p, 3)
                    pv(p, 3)
                if p.nxt:
                    xt(p)
                if p.l0:
                    ctx(p, 1)
                if p.l1:
                    to(p, 3)
                    po(p, 3)

            def head():
                pe.wait_ge(const_ok, 4)
                xt(Pass(-1, l0=False, l1=False, first=True))
                pe.wait_ge(ones_ok, 9)
                pe.wait_ge(w_lo_ok, 10)
                pe.wait_ge(b_lo, 6)

            passes(pe, body, head)


def kernel(x, adj, L0_gnn_W_left, L0_gnn_W_right, L0_gnn_W_lin, L0_gnn_b_lin, L0_gnn_ln_a, L0_gnn_ln_b,
           L1_gnn_Wq, L1_gnn_Wk, L1_gnn_Wv, L1_gnn_bv, L1_gnn_Wo, L1_gnn_bo):
    import numpy as np
    import concourse.bacc as bacc
    from concourse.bass_utils import run_bass_kernel_spmd

    def rows(w):
        return np.asarray(w).reshape(KB, 128, FEAT).transpose(1, 0, 2)

    per_layer = [(L0_gnn_W_left[l], L0_gnn_W_right[l], np.asarray(L0_gnn_W_lin[l]).T) for l in range(2)]
    l1 = [np.asarray(w).T for w in (L1_gnn_Wq, L1_gnn_Wk, L1_gnn_Wv, L1_gnn_Wo)]
    a, b = np.asarray(L0_gnn_ln_a), np.asarray(L0_gnn_ln_b)
    arrays = {
        "x": np.asarray(x),
        "adj": np.asarray(adj),
        "weights": np.stack([rows(w) for w in (*per_layer[0], *per_layer[1], *l1)]),
        "biases": np.stack([np.asarray(v) for v in (L0_gnn_b_lin[0], L0_gnn_b_lin[1], L1_gnn_bv, L1_gnn_bo)]),
        "ln_cols": np.ascontiguousarray(np.stack([a[0].reshape(KB, 128), b[0].reshape(KB, 128)]).transpose(2, 0, 1)),
        "ln_rows": np.stack([a[1], b[1]]),
    }
    nc = bacc.Bacc("TRN2", target_bir_lowering=False, num_devices=1, dynamic_dma_scratch_size=1024)
    args = [nc.dram_tensor(n, v.shape, mybir.dt.from_np(v.dtype), kind="ExternalInput").ap()
            for n, v in arrays.items()]
    out = nc.dram_tensor("out", (GRAPHS, TOK, FEAT), mybir.dt.float32, kind="ExternalOutput").ap()
    program(nc, *args, out)
    return run_bass_kernel_spmd(nc, [arrays], core_ids=[0]).results[0]["out"]
```

```python
import concourse.bass as bass
from concourse import mybir
from contextlib import ExitStack

GRAPHS, TOK, FEAT = 128, 128, 384
GROUP = 4
GROUPS = GRAPHS // GROUP
KB = FEAT // 128
HEADS = 12
HEAD = FEAT // HEADS
TILES = 128 // HEAD
GT = GROUP * TOK
VCOL = HEAD + 1
HCOL = FEAT + 2
TEMPER = float(FEAT) ** 0.5
WSCALE = 64.0
BIG = 3.0e38


class Signal:

    def __init__(self, sem, per_group):
        self.sem, self.per_group = sem, per_group

    def upto(self, group, n):
        return group * self.per_group + n


def program(nc, x, adj, weights, biases, ln_cols, ln_rows, out):
    f32, f32r, f16 = mybir.dt.float32, mybir.dt.float32r, mybir.dt.float16
    i32 = mybir.dt.int32
    ALU, ACT, AX = mybir.AluOpType, mybir.ActivationFunctionType, mybir.AxisListType
    mm, transpose = nc.tensor.matmul, nc.tensor.transpose

    with ExitStack() as stack:
        def sb(name, shape, dt=f32):
            return stack.enter_context(nc.sbuf_tensor(name, [128] + shape, dt))

        def sem(name):
            return stack.enter_context(nc.semaphore(name))

        ident = sb("ident", [128])
        keep_left = sb("keep_left", [TOK])
        keep_right = sb("keep_right", [TOK])
        ones_r = sb("ones_r", [128], f32r)
        ones_h = sb("ones_h", [128], f16)
        pw = sb("pw", [2, GROUP])
        wr_hi, wr_lo = (sb(f"wr_{p}", [6, KB, FEAT], f32r) for p in ("hi", "lo"))
        wh_hi, wh_lo = (sb(f"wh_{p}", [4, KB, FEAT], f16) for p in ("hi", "lo"))
        bias_r = sb("bias_r", [2, FEAT], f32r)
        bias_h = sb("bias_h", [2, FEAT], f16)
        lncol = sb("lncol", [2, KB])
        lnrow = sb("lnrow", [2, FEAT])
        xin = sb("xin", [GROUP, FEAT])
        xres = sb("xres", [GROUP, FEAT])
        adjn = sb("adjn", [GROUP, TOK])
        adjT = sb("adjT", [GROUP, TOK])
        mask = sb("mask", [GROUP, 2, TOK])
        hT_hi, hT_lo = (sb(f"hT_{p}", [KB, GROUP, TOK], f32r) for p in ("hi", "lo"))
        nT_hi, nT_lo = (sb(f"nT_{p}", [KB, 2, GROUP, TOK], f32r) for p in ("hi", "lo"))
        hl_hi, hl_lo = (sb(f"hl_{p}", [GROUP, HCOL], f32r) for p in ("hi", "lo"))
        uLR = sb("uLR", [2, 2, TOK])
        e = sb("e", [GROUP, TOK])
        e_hi, e_lo = (sb(f"e_{p}", [GROUP, TOK], f32r) for p in ("hi", "lo"))
        z = sb("z", [GROUP, FEAT])
        hT = sb("hT", [2, GROUP, TOK])
        x1 = sb("x1", [GROUP, FEAT])
        eps_den, rden = sb("eps_den", [GROUP]), sb("rden", [GROUP])
        st, mv = sb("st", [GROUP, 6]), sb("mv", [GROUP, 2])
        yst, ymv = sb("yst", [GROUP, 6]), sb("ymv", [GROUP, 2])
        yvar, yrstd, ynmr = sb("yvar", [GROUP]), sb("yrstd", [GROUP]), sb("ynmr", [GROUP])
        var, rstd, nmr = sb("var", [GROUP]), sb("rstd", [GROUP]), sb("nmr", [GROUP])
        sd = sb("sd", [GROUP])
        adj2 = sb("adj2", [GROUP, TOK])
        xT_hi, xT_lo = (sb(f"xT_{p}", [KB, GROUP, TOK], f16) for p in ("hi", "lo"))
        qk_hi, qk_lo = (sb(f"qk_{p}", [2, KB, GROUP, TOK], f16) for p in ("hi", "lo"))
        v_hi, v_lo = (sb(f"v_{p}", [GROUP, HEADS, VCOL], f16) for p in ("hi", "lo"))
        s = sb("s", [HEADS, TOK])
        nmax, nmin, live = sb("nmax", [HEADS]), sb("nmin", [HEADS]), sb("live", [2, HEADS])
        pT_hi, pT_lo = (sb(f"pT_{p}", [HEADS, TOK], f16) for p in ("hi", "lo"))
        rs = sb("rs", [2, HEADS])
        o = sb("o", [HEADS, HEAD])
        oT_hi, oT_lo = (sb(f"oT_{p}", [KB, TOK], f16) for p in ("hi", "lo"))
        y2 = sb("y2", [2, FEAT])
        st2, mv2 = sb("st2", [6]), sb("mv2", [2])
        var2, rstd2, nmr2 = sb("var2", [1]), sb("rstd2", [1]), sb("nmr2", [1])

        psum = stack.enter_context(nc.psum_tensor("psum", [128, 8, 512], f32))
        PJ, MX, SC = (0, 1), (2, 3), (4, 5, 6, 7)

        def signal(name, per_group):
            return Signal(sem(name), per_group)

        x_in, adj_in, xres_in = signal("x_in", 16), signal("adj_in", 16), signal("xres_in", 16)
        adj2_in = signal("adj2_in", 16)
        out_st = [signal(f"out_st{i}", 32) for i in range(2)]
        xt_full, xt_hi, xt_lo = (signal(f"xt_{p}", KB) for p in ("full", "hi", "lo"))
        adjT_full, adjT_ok, mask_ok = signal("adjT_full", 1), signal("adjT_ok", 1), signal("mask_ok", 2)
        nl_full, nl_hi, nl_lo = ([signal(f"nl{l}_{p}", 2 * KB) for l in range(2)] for p in ("full", "hi", "lo"))
        hl_full, hlr_hi, hlr_lo = ([signal(f"hl{l}_{p}", GROUP) for l in range(2)] for p in ("full", "hi", "lo"))
        u_full, u_read, u_sum, e_raw, e_ok, e_hi_ok, e_lo_ok = (
            [signal(f"{p}{l}", 2) for l in range(2)]
            for p in ("u_full", "u_read", "u_sum", "e_raw", "e_ok", "e_hi_ok", "e_lo_ok"))
        c_full, den_ok, rden_ok, z_ok, st_ok, mv_ok, n_ok = (
            [signal(f"{p}{l}", GROUP) for l in range(2)]
            for p in ("c_full", "den_ok", "rden_ok", "z_ok", "st_ok", "mv_ok", "n_ok"))
        var_ok, pow_ok, eps_ok, rstd_ok, nmr_ok = (
            [signal(f"{p}{l}", 1) for l in range(2)] for p in ("var_ok", "pow_ok", "eps_ok", "rstd_ok", "nmr_ok"))
        th_full, th_raw, th_hi, th_lo = (signal(f"th_{p}", KB) for p in ("full", "raw", "hi", "lo"))
        za_ok, zb_ok, y_ok, yst_ok, ymv_ok, x1_ok = (
            signal(p, GROUP) for p in ("za_ok", "zb_ok", "y_ok", "yst_ok", "ymv_ok", "x1_ok"))
        yvar_ok, ypow_ok, ynmr_ok = (signal(p, 1) for p in ("yvar_ok", "ypow_ok", "ynmr_ok"))
        x1t_full, x1t_hi, x1t_lo = (signal(f"x1t_{p}", KB) for p in ("full", "hi", "lo"))
        qk_full, qkr_hi, qkr_lo = (signal(f"qk_{p}", 2 * KB) for p in ("full", "hi", "lo"))
        v_full, vr_hi, vr_lo = (signal(f"v_{p}", GROUP) for p in ("full", "hi", "lo"))
        adj2_ok = signal("adj2_ok", 1)
        s_full, s_ok, s_min, p_ok = (signal(p, GROUP * TILES) for p in ("s_full", "s_ok", "s_min", "p_ok"))
        pt_full, pt_hi, pt_lo = (signal(f"pt_{p}", GROUP * KB) for p in ("full", "hi", "lo"))
        pv_full, live1, live2, rs1, rs2, o_ok = (
            signal(p, GROUP) for p in ("pv_full", "live1", "live2", "rs1", "rs2", "o_ok"))
        to_full, to_hi, to_lo = (signal(f"to_{p}", GROUP) for p in ("full", "hi", "lo"))
        po_full, y2_ok, y2st_ok, y2mv_ok, y2var_ok, y2pow_ok, y2nmr_ok, fin_ok = (
            signal(p, GROUP) for p in ("po_full", "y2_ok", "y2st_ok", "y2mv_ok", "y2var_ok", "y2pow_ok",
                                       "y2nmr_ok", "fin_ok"))
        ld, w_hi_ok, w_lo_ok, const_ok, ones_ok, b_ok, b_lo = (
            sem(p) for p in ("ld", "w_hi_ok", "w_lo_ok", "const_ok", "ones_ok", "b_ok", "b_lo"))
        w_in = [sem(f"w_in{i}") for i in range(2)]

        OF_BEFORE = (adj2_in, *out_st, za_ok, zb_ok, y_ok, yst_ok, ymv_ok, x1_ok, yvar_ok, ypow_ok, ynmr_ok,
                     x1t_full, x1t_hi, x1t_lo, qk_full, qkr_hi, qkr_lo, v_full, vr_hi, vr_lo,
                     adj2_ok, s_full, s_ok, s_min, p_ok, pt_full, pt_hi, pt_lo, pv_full, live1, live2, rs1, rs2,
                     o_ok, to_full, to_hi, to_lo, po_full, y2_ok, y2st_ok, y2mv_ok, y2var_ok, y2pow_ok,
                     y2nmr_ok, fin_ok)
        OF_NEXT = (xt_full, xt_hi, xt_lo, adjT_full, adjT_ok)

        def uses(name, parts, read):
            return [(name, i, read) for i in parts]

        PJ_ORDER = (uses("nl0", (0, 1, 2), nl_lo[0]) + uses("po", (3,), y2_ok) + uses("nl0", (3, 4, 5), nl_lo[0])
                    + uses("hl0", range(4), hlr_lo[0]) + uses("qk", range(6), qkr_lo) + uses("v", range(4), vr_lo)
                    + uses("nl1", (0, 1, 2), nl_lo[1]) + uses("po", (0,), y2_ok) + uses("nl1", (3, 4, 5), nl_lo[1])
                    + uses("hl1", (0,), hlr_lo[1]) + uses("po", (1,), y2_ok) + uses("hl1", (1, 2, 3), hlr_lo[1])
                    + uses("po", (2,), y2_ok))
        MX_ORDER = (uses("pv", (3,), o_ok) + uses("to", (3,), to_lo) + uses("x1t", range(3), x1t_lo)
                    + uses("u0", range(2), u_read[0]) + uses("c0", range(4), z_ok[0]) + uses("th", range(3), th_hi)
                    + uses("pv", (0,), o_ok) + uses("to", (0,), to_lo) + uses("pv", (1,), o_ok)
                    + uses("to", (1,), to_lo) + uses("u1", range(2), u_read[1]) + uses("pv", (2,), o_ok)
                    + uses("to", (2,), to_lo) + uses("c1", range(4), z_ok[1]) + uses("xt", range(3), xt_lo)
                    + uses("adjT", (0,), adjT_ok))
        TAIL = (("pv", 3), ("to", 3), ("po", 3))
        L1_STAGES = ("x1t", "qk", "v", "pv", "to", "po")
        NEXT_STAGES = ("xt", "adjT")

        def place(stage, i):
            for order, banks in ((PJ_ORDER, PJ), (MX_ORDER, MX)):
                for n, use in enumerate(order):
                    if use[:2] == (stage, i):
                        return order, n, banks[n % 2]

        def bank(stage, i):
            return psum[:, place(stage, i)[2], :]

        class Pass:

            def __init__(self, it, l0=True, l1=True, nxt=True, tail=True, before=None):
                self.it, self.l0, self.l1, self.nxt, self.tail, self.before = it, l0, l1, nxt, tail, before

            def has(self, use):
                if use in TAIL:
                    return self.tail
                return self.l1 if use[0] in L1_STAGES else self.nxt if use[0] in NEXT_STAGES else self.l0

            def group(self, sig):
                return self.it - 1 if sig in OF_BEFORE else self.it + 1 if sig in OF_NEXT else self.it

            def earlier(self):
                return Pass(self.it - 1)

            def await_(self, eng, sig, n):
                eng.wait_ge(sig.sem, sig.upto(self.group(sig), n))

            def await_apart(self, eng, sig, n):
                value = sig.upto(self.group(sig), n)
                if not isinstance(value, int):
                    value = eng.snap(eng.to_reg(value), min_val=1)
                eng.wait_ge(sig.sem, 1)
                eng.wait_ge(sig.sem, value)

            def await_bank(self, eng, stage, i):
                order, n, _ = place(stage, i)
                candidates = [(self, m) for m in range(n - 2, -1, -2)]
                if self.before:
                    candidates += [(self.before, m) for m in range(len(order) - 1, -1, -1) if m % 2 == n % 2]
                for run, m in candidates:
                    name, j, read = order[m]
                    if run.has((name, j)):
                        group = run.group(read) - (1 if (name, j) in TAIL else 0)
                        eng.wait_ge(read.sem, read.upto(group, j + 1))
                        return

        def passes(eng, body, head=None):
            if head:
                head()
            first = Pass(0, l1=False, tail=False)
            body(first)
            body(Pass(1, tail=False, before=first))
            with eng.Fori(2, GROUPS - 1) as it:
                body(Pass(it, before=Pass(it - 1)))
            body(Pass(GROUPS - 1, nxt=False, before=Pass(GROUPS - 2)))
            body(Pass(GROUPS, l0=False, nxt=False, before=Pass(GROUPS - 1, nxt=False)))
            body(Pass(GROUPS + 1, l0=False, l1=False, nxt=False, before=Pass(GROUPS, l0=False, nxt=False)))

        prologue = Pass(-1, l0=False, l1=False, tail=False)

        stage_w = [z[:, 0:KB], x1[:, 0:KB]]
        stage_b = s[:].rearrange("p (a h) t -> p a (h t)", a=4)

        block = stack.enter_context(nc.Block())

        @block.sync
        def _(sp):
            for m in range(10):
                if m >= 2:
                    sp.wait_ge(w_lo_ok, m - 1)
                sp.dma_start(stage_w[m % 2], weights[m]).then_inc(w_in[m % 2], 16)
                if m == 1:
                    sp.dma_start(xin[:], x[0:GROUP].rearrange("b t f -> t b f")).then_inc(x_in.sem, 16)
                    sp.dma_start(adjn[:], adj[0:GROUP].rearrange("b i j -> i b j")).then_inc(adj_in.sem, 16)
            sp.dma_start(lncol[:], ln_cols).then_inc(ld, 16)
            sp.dma_start(lnrow[:], ln_rows.rearrange("a f -> (a f)")[None, :].to_broadcast([128, 2 * FEAT])).then_inc(ld, 16)
            sp.wait_ge(const_ok, 1)
            for half in range(2):
                sp.dma_start(stage_b[32 * half:32 * half + 1, :, :], biases[None, :, :]).then_inc(ld, 16)

            def store(p, b):
                p.await_(sp, fin_ok, b + 1)
                sp.dma_start(out[bass.ds((p.it - 1) * GROUP + b, 1)].rearrange("b t f -> t (b f)"), y2[:, b % 2])\
                    .then_inc(out_st[b % 2].sem, 16)

            def body(p):
                it = p.it
                if p.l1:
                    if p.before.l1:
                        p.before.await_(sp, s_ok, GROUP * TILES)
                    sp.dma_start(adj2[:], adj[bass.ds((it - 1) * GROUP, GROUP)].rearrange("b i j -> i b j"))\
                        .then_inc(adj2_in.sem, 16)
                if p.nxt:
                    sp.wait_ge(xt_full.sem, xt_full.upto(it, KB))
                    sp.dma_start(xin[:], x[bass.ds((it + 1) * GROUP, GROUP)].rearrange("b t f -> t b f"))\
                        .then_inc(x_in.sem, 16)
                    sp.wait_ge(adjT_full.sem, adjT_full.upto(it, 1))
                    sp.wait_ge(mask_ok.sem, mask_ok.upto(it, 2))
                    sp.dma_start(adjn[:], adj[bass.ds((it + 1) * GROUP, GROUP)].rearrange("b i j -> i b j"))\
                        .then_inc(adj_in.sem, 16)
                if p.tail:
                    store(p.earlier(), 3)
                if p.l0:
                    if p.l1:
                        p.await_(sp, y_ok, GROUP)
                    sp.dma_start(xres[:], x[bass.ds(it * GROUP, GROUP)].rearrange("b t f -> t b f"))\
                        .then_inc(xres_in.sem, 16)
                if p.l1:
                    for b in range(3):
                        store(p, b)

            passes(sp, body)
            for i in range(2):
                sp.wait_ge(out_st[i].sem, out_st[i].upto(GROUPS - 1, 32))

        @block.gpsimd
        def _(pool):
            nc.gpsimd.memset(stage_b[:], 0.0).then_inc(const_ok, 1)
            nc.gpsimd.memset(ident[:], 0.0).then_inc(b_ok, 1)
            nc.gpsimd.memset(keep_left[:], 1.0 / TEMPER).then_inc(b_ok, 1)
            nc.gpsimd.memset(keep_right[:], 1.0 / TEMPER).then_inc(b_ok, 1)
            nc.gpsimd.memset(pw[:, 0], 0.5).then_inc(ones_ok, 1)
            nc.gpsimd.memset(pw[:, 1], -0.5).then_inc(ones_ok, 1)
            nc.gpsimd.memset(ones_r[:].bitcast(f32), 1.0).then_inc(ones_ok, 1)
            nc.gpsimd.memset(ones_h[:], 1.0).then_inc(ones_ok, 1)
            nc.gpsimd.memset(hl_hi[:, :, FEAT:FEAT + 1].bitcast(f32), 1.0).then_inc(ones_ok, 1)
            nc.gpsimd.memset(hl_hi[:, :, FEAT + 1:HCOL].bitcast(f32), 0.0).then_inc(ones_ok, 1)
            nc.gpsimd.memset(hl_lo[:, :, FEAT:HCOL].bitcast(f32), 0.0).then_inc(ones_ok, 1)
            nc.gpsimd.memset(v_hi[:, :, :, HEAD:VCOL], 1.0).then_inc(ones_ok, 1)
            nc.gpsimd.memset(v_lo[:, :, :, HEAD:VCOL], 0.0).then_inc(ones_ok, 1)
            pool.wait_ge(b_ok, 3)
            nc.gpsimd.affine_select(out=ident[:], in_=ident[:], compare_op=ALU.not_equal, fill=1.0, base=0,
                                    pattern=[[-1, 128]], channel_multiplier=1).then_inc(const_ok, 1)
            nc.gpsimd.affine_select(out=keep_left[:], in_=keep_left[:], compare_op=ALU.is_ge, fill=0.0, base=0,
                                    pattern=[[-1, TOK]], channel_multiplier=1).then_inc(const_ok, 1)
            nc.gpsimd.affine_select(out=keep_right[:], in_=keep_right[:], compare_op=ALU.is_gt, fill=0.0, base=0,
                                    pattern=[[1, TOK]], channel_multiplier=-1).then_inc(const_ok, 1)
            pool.wait_ge(const_ok, 4)
            pool.wait_ge(ones_ok, 9)

            def masks(p, sig_group):
                pool.wait_ge(adj_in.sem, adj_in.upto(sig_group, 16))
                pool.wait_ge(adjT_ok.sem, adjT_ok.upto(sig_group, 1))
                if p is not None:
                    p.await_(pool, u_read[1], 2)
                nc.gpsimd.tensor_tensor(mask[:, :, 0], adjT[:], keep_L, ALU.mult).then_inc(mask_ok.sem, 1)
                nc.gpsimd.tensor_tensor(mask[:, :, 1], adjn[:], keep_R, ALU.mult).then_inc(mask_ok.sem, 1)

            keep_L = keep_left[:, None, :].to_broadcast([128, GROUP, TOK])
            keep_R = keep_right[:, None, :].to_broadcast([128, GROUP, TOK])

            def weigh(p, l):
                for h in range(2):
                    part = slice(2 * h, 2 * h + 2)
                    p.await_(pool, e_raw[l], h + 1)
                    nc.gpsimd.tensor_tensor(e[:, part], e[:, part], adjT[:, part], ALU.mult).then_inc(e_ok[l].sem, 1)
                for h in range(2):
                    part = slice(2 * h, 2 * h + 2)
                    p.await_(pool, e_hi_ok[l], h + 1)
                    p.await_(pool, e_ok[l], h + 1)
                    nc.gpsimd.tensor_tensor(e_lo[:, part], e[:, part], e_hi[:, part].bitcast(f32), ALU.subtract)\
                        .then_inc(e_lo_ok[l].sem, 1)

            def power(p, src_ok, dst, src, exponent, done, n=1):
                p.await_(pool, src_ok, n)
                w = dst.shape[-1]
                nc.gpsimd.tensor_tensor(dst, src, pw[:, exponent, 0:w], ALU.pow).then_inc(done.sem, 1)

            def y2_power(p, b):
                power(p, y2var_ok, rstd2[:], var2[:], 1, y2pow_ok, b + 1)

            def body(p):
                if p.l1:
                    for b in range(GROUP):
                        p.before.await_(pool, n_ok[1], b + 1)
                        nc.gpsimd.tensor_tensor(z[:, b], z[:, b], lnrow[:, 0], ALU.mult).then_inc(za_ok.sem, 1)
                        p.await_(pool, za_ok, b + 1)
                        nc.gpsimd.tensor_tensor(z[:, b], z[:, b], lnrow[:, 1], ALU.add).then_inc(zb_ok.sem, 1)
                if p.tail:
                    y2_power(p.earlier(), 3)
                if p.l1:
                    power(p, yvar_ok, yrstd[:], yvar[:], 1, ypow_ok)
                if p.l0:
                    weigh(p, 0)
                if p.l1:
                    p.await_apart(pool, adj2_in, 16)
                    nc.gpsimd.tensor_scalar(adj2[:], adj2[:], 2.0, TEMPER, ALU.mult, ALU.mult)\
                        .then_inc(adj2_ok.sem, 1)
                if p.l0:
                    power(p, var_ok[0], sd[:], var[:], 0, pow_ok[0])
                if p.l1:
                    y2_power(p, 0)
                if p.l0:
                    weigh(p, 1)
                if p.l1:
                    y2_power(p, 1)
                if p.l0:
                    power(p, var_ok[1], sd[:], var[:], 0, pow_ok[1])
                if p.l1:
                    y2_power(p, 2)
                if p.nxt:
                    masks(p, p.it + 1)

            def head():
                pool.wait_ge(ld, 64)
                masks(None, 0)

            passes(pool, body, head)

        @block.scalar
        def _(act):
            def copy(dst, src, scale=1.0):
                return nc.scalar.activation(dst, src, ACT.Copy, scale=scale)

            def hi(p, full, n, stage, dst, done, scale=1.0):
                p.await_(act, full, n + 1)
                w = 1
                for d in dst.shape[1:]:
                    w *= d
                src = bank(stage, n)[:, 0:w]
                if len(dst.shape) == 3:
                    src = src.rearrange("p (a b) -> p a b", a=dst.shape[1])
                copy(dst, src, scale).then_inc(done.sem, 1)

            def xt(p):
                for k in range(KB):
                    hi(p, xt_full, k, "xt", hT_hi[:, k], xt_hi)
                p.await_(act, adjT_full, 1)
                if p.l0:
                    p.await_(act, e_ok[1], 2)
                copy(adjT[:], bank("adjT", 0).rearrange("p (a b) -> p a b", a=GROUP)).then_inc(adjT_ok.sem, 1)

            def nl(p, l, c):
                if p.l0:
                    lr, kb = divmod(c, KB)
                    hi(p, nl_full[l], c, f"nl{l}", nT_hi[:, kb, lr], nl_hi[l])

            def hl(p, l, b):
                if p.l0:
                    hi(p, hl_full[l], b, f"hl{l}", hl_hi[:, b, 0:FEAT], hlr_hi[l])

            def v(p, b):
                p.await_(act, v_full, b + 1)
                copy(v_hi[:, b, :, 0:HEAD], bank("v", b)[:, 0:FEAT].rearrange("p (h d) -> p h d", h=HEADS),
                     1.0 / WSCALE).then_inc(vr_hi.sem, 1)

            def exps(p, b, j):
                if not p.l1:
                    return
                p.await_(act, s_min, b * TILES + j + 1)
                for c in range(KB):
                    h = TILES * c + j
                    last = nc.scalar.activation(s[:, h], s[:, h], ACT.Exp, bias=nmax[:, h:h + 1], scale=-1.0)
                last.then_inc(p_ok.sem, 1)

            def exp_u(p, l, h):
                if p.l0:
                    p.await_(act, u_sum[l], h + 1)
                    nc.scalar.activation(e[:, 2 * h:2 * h + 2], e[:, 2 * h:2 * h + 2], ACT.Exp).then_inc(e_raw[l].sem, 1)

            def round_e(p, l, h):
                if p.l0:
                    p.await_(act, e_ok[l], h + 1)
                    copy(e_hi[:, 2 * h:2 * h + 2], e[:, 2 * h:2 * h + 2]).then_inc(e_hi_ok[l].sem, 1)

            def pt(p, b):
                if p.l1:
                    for c in range(KB):
                        p.await_(act, pt_full, b * KB + c + 1)
                        copy(pT_hi[:, TILES * c:TILES * (c + 1)],
                             psum[:, SC[c], :].rearrange("p (a b) -> p a b", a=TILES)).then_inc(pt_hi.sem, 1)

            def ctx(p, l, b):
                if p.l0:
                    p.await_(act, rden_ok[l], b + 1)
                    copy(z[:, b], bank(f"c{l}", b)[:, 0:FEAT], scale=rden[:, b:b + 1]).then_inc(z_ok[l].sem, 1)

            def th(p, k):
                if not p.l0:
                    return
                p.await_(act, th_full, k + 1)
                src = bank("th", k).rearrange("p (a b) -> p a b", a=GROUP)
                if k == 2:
                    p.await_(act, th_lo, 1)
                for dst, done in ((hT[:, k % 2], th_raw), (hT_hi[:, k], th_hi)):
                    nc.scalar.activation(dst, src, ACT.Relu, bias=lncol[:, 1, k:k + 1], scale=lncol[:, 0, k:k + 1])\
                        .then_inc(done.sem, 1)

            def to(p, b):
                hi(p, to_full, b, "to", oT_hi[:], to_hi)

            def body(p):
                nl(p, 0, 0)
                nl(p, 0, 1)
                if p.tail:
                    to(p.earlier(), 3)
                for c in range(2, 2 * KB):
                    nl(p, 0, c)
                if p.l1:
                    for k in range(KB):
                        hi(p, x1t_full, k, "x1t", xT_hi[:, k], x1t_hi)
                exp_u(p, 0, 0)
                exp_u(p, 0, 1)
                hl(p, 0, 0)
                hl(p, 0, 1)
                round_e(p, 0, 0)
                hl(p, 0, 2)
                round_e(p, 0, 1)
                hl(p, 0, 3)
                for b in range(GROUP):
                    ctx(p, 0, b)
                if p.l1:
                    for c in range(2 * KB):
                        hi(p, qk_full, c, "qk", qk_hi[:, c // KB, c % KB], qkr_hi, 1.0 / WSCALE)
                th(p, 0)
                exps(p, 0, 0)
                th(p, 1)
                exps(p, 0, 1)
                th(p, 2)
                if p.l1:
                    v(p, 0)
                    exps(p, 0, 2)
                    v(p, 1)
                    exps(p, 0, 3)
                    v(p, 2)
                    v(p, 3)
                pt(p, 0)
                nl(p, 1, 0)
                exps(p, 1, 0)
                nl(p, 1, 1)
                if p.l1:
                    to(p, 0)
                exps(p, 1, 1)
                exps(p, 1, 2)
                nl(p, 1, 2)
                exps(p, 1, 3)
                nl(p, 1, 3)
                nl(p, 1, 4)
                pt(p, 1)
                nl(p, 1, 5)
                exps(p, 2, 0)
                hl(p, 1, 0)
                if p.l1:
                    to(p, 1)
                exps(p, 2, 1)
                exp_u(p, 1, 0)
                exps(p, 2, 2)
                exp_u(p, 1, 1)
                exps(p, 2, 3)
                round_e(p, 1, 0)
                hl(p, 1, 1)
                round_e(p, 1, 1)
                pt(p, 2)
                hl(p, 1, 2)
                exps(p, 3, 0)
                hl(p, 1, 3)
                if p.l1:
                    to(p, 2)
                exps(p, 3, 1)
                ctx(p, 1, 0)
                ctx(p, 1, 1)
                exps(p, 3, 2)
                ctx(p, 1, 2)
                ctx(p, 1, 3)
                exps(p, 3, 3)
                if p.nxt:
                    xt(p)
                pt(p, 3)

            def head():
                for m in range(10):
                    act.wait_ge(w_in[m % 2], 16 * (m // 2 + 1))
                    if m < 6:
                        copy(wr_hi[:, m], stage_w[m % 2]).then_inc(w_hi_ok, 1)
                    else:
                        copy(wh_hi[:, m - 6], stage_w[m % 2], WSCALE).then_inc(w_hi_ok, 1)
                xt(prologue)

            passes(act, body, head)

        @block.vector
        def _(dve):
            def lo(p, hi_ok, n, stage, dst, rounded, done, scale=None):
                p.await_(dve, hi_ok, n + 1)
                w = 1
                for d in dst.shape[1:]:
                    w *= d
                src = bank(stage, n)[:, 0:w]
                if len(dst.shape) == 3:
                    src = src.rearrange("p (a b) -> p a b", a=dst.shape[1])
                if scale is None:
                    nc.vector.tensor_tensor(dst, src, rounded, ALU.subtract).then_inc(done.sem, 1)
                else:
                    nc.vector.scalar_tensor_tensor(dst, src, scale, rounded, ALU.mult, ALU.subtract)\
                        .then_inc(done.sem, 1)

            def xt(p):
                for k in range(KB):
                    lo(p, xt_hi, k, "xt", hT_lo[:, k], hT_hi[:, k].bitcast(f32), xt_lo)

            def nl(p, l, *cs):
                for c in cs if p.l0 else ():
                    lr, kb = divmod(c, KB)
                    lo(p, nl_hi[l], c, f"nl{l}", nT_lo[:, kb, lr], nT_hi[:, kb, lr].bitcast(f32), nl_lo[l])

            def hl(p, l, b):
                if p.l0:
                    lo(p, hlr_hi[l], b, f"hl{l}", hl_lo[:, b, 0:FEAT], hl_hi[:, b, 0:FEAT].bitcast(f32), hlr_lo[l])

            def scores(p, b, j):
                if not p.l1:
                    return
                if b == 0 and j == 0:
                    p.await_apart(dve, adj2_ok, 1)
                p.await_apart(dve, s_full, b * TILES + j + 1)
                for c in range(KB):
                    h = TILES * c + j
                    last = nc.vector.tensor_tensor_reduce(
                        out=s[:, h], in0=psum[:, SC[j], c * TOK:(c + 1) * TOK], in1=adj2[:, b],
                        scale=-1.0 / TEMPER, scalar=BIG, op0=ALU.add, op1=ALU.min, accum_out=nmax[:, h:h + 1])
                last.then_inc(s_ok.sem, 1)
                p.await_(dve, s_ok, b * TILES + j + 1)
                nc.vector.tensor_reduce(nmin[:, j::TILES], s[:, j::TILES], AX.X, ALU.max).then_inc(s_min.sem, 1)

            def guard(p, b):
                if not p.l1:
                    return
                p.await_(dve, s_min, (b + 1) * TILES)
                nc.vector.tensor_scalar(live[:, 0], nmax[:], 0.0, None, ALU.not_equal).then_inc(live1.sem, 1)
                p.await_(dve, live1, b + 1)
                nc.vector.scalar_tensor_tensor(live[:, 1], nmin[:], 0.0, live[:, 0], ALU.not_equal, ALU.max)\
                    .then_inc(live2.sem, 1)

            def pt(p, b):
                for c in range(KB) if p.l1 else ():
                    p.await_(dve, pt_hi, b * KB + c + 1)
                    hs = slice(TILES * c, TILES * (c + 1))
                    nc.vector.tensor_tensor(pT_lo[:, hs], psum[:, SC[c], :].rearrange("p (a b) -> p a b", a=TILES),
                                            pT_hi[:, hs], ALU.subtract).then_inc(pt_lo.sem, 1)

            def pv(p, b):
                src = bank("pv", b)[:, 0:HEADS * VCOL].rearrange("p (h d) -> p h d", h=HEADS)
                p.await_(dve, pv_full, b + 1)
                nc.vector.reciprocal(rs[:, 0], src[:, :, HEAD]).then_inc(rs1.sem, 1)
                p.await_(dve, rs1, b + 1)
                p.await_(dve, live2, b + 1)
                nc.vector.tensor_tensor(rs[:, 1], rs[:, 0], live[:, 1], ALU.mult).then_inc(rs2.sem, 1)
                p.await_(dve, rs2, b + 1)
                nc.vector.tensor_tensor(o[:], src[:, :, 0:HEAD],
                                        rs[:, 1, :, None].to_broadcast([128, HEADS, HEAD]), ALU.mult)\
                    .then_inc(o_ok.sem, 1)

            def to(p, b):
                lo(p, to_hi, b, "to", oT_lo[:], oT_hi[:], to_lo)

            def po(p, b):
                p.await_(dve, po_full, b + 1)
                if b >= 2:
                    p.await_(dve, out_st[b % 2], 16)
                elif p.tail:
                    p.before.await_(dve, out_st[b % 2], 32)
                nc.vector.scalar_tensor_tensor(y2[:, b % 2], bank("po", b)[:, 0:FEAT], 1.0 / WSCALE, x1[:, b],
                                               ALU.mult, ALU.add).then_inc(y2_ok.sem, 1)
                p.await_(dve, y2_ok, b + 1)
                nc.vector.bn_stats(st2[:], y2[:, b % 2]).then_inc(y2st_ok.sem, 1)
                p.await_apart(dve, y2st_ok, b + 1)
                nc.vector.bn_aggr(mv2[:], st2[:]).then_inc(y2mv_ok.sem, 1)
                p.await_(dve, y2mv_ok, b + 1)
                nc.vector.tensor_scalar(var2[:], mv2[:, 1:2], 1e-5, None, ALU.add).then_inc(y2var_ok.sem, 1)

            def fin(p, b):
                p.await_(dve, y2pow_ok, b + 1)
                nc.vector.scalar_tensor_tensor(nmr2[:], mv2[:, 0:1], -1.0, rstd2[:], ALU.mult, ALU.mult)\
                    .then_inc(y2nmr_ok.sem, 1)
                p.await_(dve, y2nmr_ok, b + 1)
                nc.vector.tensor_scalar(y2[:, b % 2], y2[:, b % 2], rstd2[:], nmr2[:], ALU.mult, ALU.add)\
                    .then_inc(fin_ok.sem, 1)

            def u(p, l, h):
                if not p.l0:
                    return
                p.await_(dve, u_full[l], h + 1)
                if h == 1:
                    p.await_(dve, u_sum[l], 1)
                if l == 0 and h == 0:
                    dve.wait_ge(mask_ok.sem, mask_ok.upto(p.it, 2))
                nc.vector.tensor_tensor(uLR[:], bank(f"u{l}", h).rearrange("p (b r t) -> p b r t", b=2, r=2),
                                        mask[:, 2 * h:2 * h + 2], ALU.mult).then_inc(u_read[l].sem, 1)
                p.await_(dve, u_read[l], h + 1)
                nc.vector.tensor_tensor(e[:, 2 * h:2 * h + 2], uLR[:, :, 0], uLR[:, :, 1], ALU.add)\
                    .then_inc(u_sum[l].sem, 1)

            def den(p, l, b):
                if not p.l0:
                    return
                p.await_(dve, c_full[l], b + 1)
                nc.vector.tensor_scalar(eps_den[:, b:b + 1], bank(f"c{l}", b)[:, FEAT:FEAT + 1], 1e-10, None, ALU.add)\
                    .then_inc(den_ok[l].sem, 1)
                p.await_(dve, den_ok[l], b + 1)
                nc.vector.reciprocal(rden[:, b:b + 1], eps_den[:, b:b + 1]).then_inc(rden_ok[l].sem, 1)

            def stats(p, src, src_ok, st, mv, var, st_done, mv_done, var_done, factor, eps):
                for b in range(GROUP):
                    p.await_(dve, src_ok, b + 1)
                    nc.vector.bn_stats(st[:, b], src[:, b]).then_inc(st_done.sem, 1)
                for b in range(GROUP):
                    p.await_apart(dve, st_done, b + 1)
                    nc.vector.bn_aggr(mv[:, b], st[:, b]).then_inc(mv_done.sem, 1)
                p.await_(dve, mv_done, GROUP)
                nc.vector.tensor_scalar(var[:], mv[:, :, 1], factor, eps, ALU.mult, ALU.add).then_inc(var_done.sem, 1)

            def norm(p, l):
                p.await_(dve, pow_ok[l], 1)
                nc.vector.tensor_scalar(var[:], sd[:], 1e-3, None, ALU.add).then_inc(eps_ok[l].sem, 1)
                p.await_(dve, eps_ok[l], 1)
                nc.vector.reciprocal(rstd[:], var[:]).then_inc(rstd_ok[l].sem, 1)
                p.await_(dve, rstd_ok[l], 1)
                nc.vector.scalar_tensor_tensor(nmr[:], mv[:, :, 0], -1.0, rstd[:], ALU.mult, ALU.mult)\
                    .then_inc(nmr_ok[l].sem, 1)
                p.await_(dve, nmr_ok[l], 1)

            def norm_z(p, l, *bs):
                for b in bs if p.l0 else ():
                    nc.vector.tensor_scalar(z[:, b], z[:, b], rstd[:, b:b + 1], nmr[:, b:b + 1], ALU.mult, ALU.add)\
                        .then_inc(n_ok[l].sem, 1)

            def th(p, k):
                p.await_(dve, th_hi, k + 1)
                nc.vector.tensor_tensor(hT_lo[:, k], hT[:, k % 2], hT_hi[:, k].bitcast(f32), ALU.subtract)\
                    .then_inc(th_lo.sem, 1)

            def resid(p, b):
                if p.l1:
                    if b == 0:
                        p.before.await_(dve, xres_in, 16)
                    p.await_(dve, zb_ok, b + 1)
                    nc.vector.scalar_tensor_tensor(x1[:, b], z[:, b], 0.0, xres[:, b], ALU.max, ALU.add)\
                        .then_inc(y_ok.sem, 1)

            def resid_norm(p):
                p.await_(dve, ypow_ok, 1)
                nc.vector.scalar_tensor_tensor(ynmr[:], ymv[:, :, 0], -1.0, yrstd[:], ALU.mult, ALU.mult)\
                    .then_inc(ynmr_ok.sem, 1)
                p.await_(dve, ynmr_ok, 1)
                for b in range(GROUP):
                    nc.vector.tensor_scalar(x1[:, b], x1[:, b], yrstd[:, b:b + 1], ynmr[:, b:b + 1], ALU.mult, ALU.add)\
                        .then_inc(x1_ok.sem, 1)

            def v(p, b):
                p.await_(dve, vr_hi, b + 1)
                nc.vector.scalar_tensor_tensor(
                    v_lo[:, b, :, 0:HEAD], bank("v", b)[:, 0:FEAT].rearrange("p (h d) -> p h d", h=HEADS),
                    1.0 / WSCALE, v_hi[:, b, :, 0:HEAD], ALU.mult, ALU.subtract).then_inc(vr_lo.sem, 1)

            def qk(p, *cs):
                for c in cs if p.l1 else ():
                    lo(p, qkr_hi, c, "qk", qk_lo[:, c // KB, c % KB], qk_hi[:, c // KB, c % KB], qkr_lo, 1.0 / WSCALE)

            def z_stats(p, l):
                if p.l0:
                    stats(p, z, z_ok[l], st, mv, var, st_ok[l], mv_ok[l], var_ok[l], FEAT / (FEAT - 1.0), 0.0)

            def z_norm(p, l):
                if p.l0:
                    norm(p, l)

            def body(p):
                tail = p.earlier()
                nl(p, 0, 0)
                if p.tail:
                    pv(tail, 3)
                nl(p, 0, 1)
                resid(p, 0)
                if p.tail:
                    to(tail, 3)
                nl(p, 0, 2)
                resid(p, 1)
                if p.tail:
                    po(tail, 3)
                resid(p, 2)
                nl(p, 0, 3)
                resid(p, 3)
                if p.tail:
                    fin(tail, 3)
                if p.l1:
                    stats(p, x1, y_ok, yst, ymv, yvar, yst_ok, ymv_ok, yvar_ok, 1.0, 1e-5)
                nl(p, 0, 4)
                if p.l1:
                    resid_norm(p)
                nl(p, 0, 5)
                if p.l1:
                    for k in range(KB):
                        lo(p, x1t_hi, k, "x1t", xT_lo[:, k], xT_hi[:, k], x1t_lo)
                u(p, 0, 0)
                u(p, 0, 1)
                for b in range(GROUP):
                    hl(p, 0, b)
                for b in range(GROUP):
                    den(p, 0, b)
                qk(p, 0)
                z_stats(p, 0)
                qk(p, 1, 2)
                z_norm(p, 0)
                norm_z(p, 0, 0, 1)
                qk(p, 3)
                norm_z(p, 0, 2, 3)
                qk(p, 4, 5)
                scores(p, 0, 0)
                scores(p, 0, 1)
                if p.l0:
                    th(p, 0)
                scores(p, 0, 2)
                if p.l0:
                    th(p, 1)
                scores(p, 0, 3)
                if p.l0:
                    th(p, 2)
                guard(p, 0)
                if p.l1:
                    for b in range(GROUP):
                        v(p, b)
                pt(p, 0)
                nl(p, 1, 0)
                if p.l1:
                    pv(p, 0)
                scores(p, 1, 0)
                scores(p, 1, 1)
                nl(p, 1, 1)
                if p.l1:
                    to(p, 0)
                scores(p, 1, 2)
                scores(p, 1, 3)
                nl(p, 1, 2)
                guard(p, 1)
                if p.l1:
                    po(p, 0)
                nl(p, 1, 3)
                nl(p, 1, 4)
                if p.l1:
                    fin(p, 0)
                pt(p, 1)
                nl(p, 1, 5)
                if p.l1:
                    pv(p, 1)
                scores(p, 2, 0)
                hl(p, 1, 0)
                scores(p, 2, 1)
                if p.l1:
                    to(p, 1)
                scores(p, 2, 2)
                u(p, 1, 0)
                scores(p, 2, 3)
                u(p, 1, 1)
                guard(p, 2)
                if p.l1:
                    po(p, 1)
                hl(p, 1, 1)
                pt(p, 2)
                hl(p, 1, 2)
                if p.l1:
                    fin(p, 1)
                    pv(p, 2)
                scores(p, 3, 0)
                hl(p, 1, 3)
                scores(p, 3, 1)
                if p.l1:
                    to(p, 2)
                den(p, 1, 0)
                den(p, 1, 1)
                scores(p, 3, 2)
                den(p, 1, 2)
                den(p, 1, 3)
                scores(p, 3, 3)
                guard(p, 3)
                if p.l1:
                    po(p, 2)
                z_stats(p, 1)
                if p.nxt:
                    xt(p)
                z_norm(p, 1)
                norm_z(p, 1, 0, 1, 2, 3)
                if p.l1:
                    fin(p, 2)
                pt(p, 3)

            def head():
                for m in range(10):
                    dve.wait_ge(w_hi_ok, m + 1)
                    if m < 6:
                        nc.vector.tensor_tensor(wr_lo[:, m], stage_w[m % 2], wr_hi[:, m].bitcast(f32), ALU.subtract)\
                            .then_inc(w_lo_ok, 1)
                    else:
                        nc.vector.scalar_tensor_tensor(wh_lo[:, m - 6], stage_w[m % 2], WSCALE, wh_hi[:, m - 6],
                                                       ALU.mult, ALU.subtract).then_inc(w_lo_ok, 1)
                dve.wait_ge(ld, 64)
                nc.vector.tensor_copy(bias_r[:], stage_b[:, 0:2]).then_inc(b_lo, 1)
                nc.vector.tensor_scalar(bias_h[:], stage_b[:, 2:4], WSCALE, None, ALU.mult).then_inc(b_lo, 1)
                dve.wait_ge(b_lo, 2)
                rows = slice(32, 64)
                nc.vector.tensor_tensor(stage_b[rows, 0:2], stage_b[rows, 0:2], bias_r[rows].bitcast(f32), ALU.subtract)\
                    .then_inc(b_lo, 1)
                nc.vector.scalar_tensor_tensor(stage_b[rows, 2:4], stage_b[rows, 2:4], WSCALE, bias_h[rows],
                                               ALU.mult, ALU.subtract).then_inc(b_lo, 1)
                dve.wait_ge(b_lo, 4)
                nc.vector.tensor_copy(bias_r[rows], stage_b[rows, 0:2]).then_inc(b_lo, 1)
                nc.vector.tensor_copy(bias_h[rows], stage_b[rows, 2:4]).then_inc(b_lo, 1)
                dve.wait_ge(b_lo, 6)
                xt(prologue)

            passes(dve, body, head)

        @block.tensor
        def _(pe):
            def product(dst, terms, done, n=1):
                total = len(terms)
                for i, (a, b) in enumerate(terms):
                    last = mm(dst, a, b, start=(i == 0), stop=(i == total - 1))
                last.then_inc(done.sem, n)

            def split(a_hi, a_lo, b_hi, b_lo):
                return [(a_hi, b_hi), (a_hi, b_lo), (a_lo, b_hi)]

            def turn(stage, i, srcs, done):
                dst = bank(stage, i)
                for n, src in enumerate(srcs):
                    last = transpose(dst[:, n * 128:(n + 1) * 128], src, ident[:])
                last.then_inc(done.sem, 1)

            def xt(p):
                pe.wait_ge(x_in.sem, x_in.upto(p.it + 1, 16))
                for k in range(KB):
                    p.await_bank(pe, "xt", k)
                    turn("xt", k, [xin[:, b, k * 128:(k + 1) * 128] for b in range(GROUP)], xt_full)
                pe.wait_ge(adj_in.sem, adj_in.upto(p.it + 1, 16))
                p.await_bank(pe, "adjT", 0)
                turn("adjT", 0, [adjn[:, b] for b in range(GROUP)], adjT_full)

            def nl(p, l, *cs):
                for c in cs if p.l0 else ():
                    lr, kb = divmod(c, KB)
                    p.await_bank(pe, f"nl{l}", c)
                    w = slice(kb * 128, (kb + 1) * 128)
                    product(bank(f"nl{l}", c), [t for k in range(KB) for t in split(
                        wr_hi[:, 3 * l + lr, k, w], wr_lo[:, 3 * l + lr, k, w],
                        hT_hi[:, k].rearrange("p b t -> p (b t)"), hT_lo[:, k].rearrange("p b t -> p (b t)"))],
                        nl_full[l])

            def hl(p, l, *bs):
                for b in bs if p.l0 else ():
                    p.await_bank(pe, f"hl{l}", b)
                    product(bank(f"hl{l}", b)[:, 0:FEAT], [t for k in range(KB) for t in split(
                        hT_hi[:, k, b], hT_lo[:, k, b], wr_hi[:, 3 * l + 2, k], wr_lo[:, 3 * l + 2, k])]
                        + [(ones_r[:], bias_r[:, l])], hl_full[l])

            def u(p, l):
                if not p.l0:
                    return
                p.await_(pe, nl_lo[l], 2 * KB)
                for h in range(2):
                    p.await_bank(pe, f"u{l}", h)
                    for g in range(2):
                        b = 2 * h + g
                        dst = bank(f"u{l}", h)[:, g * 256:(g + 1) * 256].rearrange("p (r t) -> p r t", r=2)
                        terms = [t for k in range(KB) for t in split(
                            hT_hi[:, k, b], hT_lo[:, k, b], nT_hi[:, k, :, b], nT_lo[:, k, :, b])]
                        for i, (a, m) in enumerate(terms):
                            last = mm(dst, a, m, start=(i == 0), stop=(i == len(terms) - 1))
                    last.then_inc(u_full[l].sem, 1)

            def ctx(p, l):
                if not p.l0:
                    return
                p.await_(pe, hlr_lo[l], GROUP)
                for b in range(GROUP):
                    if b % 2 == 0:
                        p.await_(pe, e_lo_ok[l], b // 2 + 1)
                    p.await_bank(pe, f"c{l}", b)
                    product(bank(f"c{l}", b)[:, 0:HCOL], split(e_hi[:, b], e_lo[:, b], hl_hi[:, b], hl_lo[:, b]),
                            c_full[l])

            def th(p):
                p.await_(pe, n_ok[0], GROUP)
                for k in range(KB):
                    p.await_bank(pe, "th", k)
                    turn("th", k, [z[:, b, k * 128:(k + 1) * 128] for b in range(GROUP)], th_full)

            def x1t(p):
                p.await_(pe, x1_ok, GROUP)
                for k in range(KB):
                    p.await_bank(pe, "x1t", k)
                    turn("x1t", k, [x1[:, b, k * 128:(k + 1) * 128] for b in range(GROUP)], x1t_full)

            def qk(p):
                p.await_(pe, x1t_lo, KB)
                for c in range(2 * KB):
                    p.await_bank(pe, "qk", c)
                    w = slice((c % KB) * 128, (c % KB + 1) * 128)
                    product(bank("qk", c), [t for k in range(KB) for t in split(
                        wh_hi[:, c // KB, k, w], wh_lo[:, c // KB, k, w],
                        xT_hi[:, k].rearrange("p b t -> p (b t)"), xT_lo[:, k].rearrange("p b t -> p (b t)"))],
                        qk_full)

            def v(p):
                for b in range(GROUP):
                    p.await_bank(pe, "v", b)
                    product(bank("v", b)[:, 0:FEAT], [t for k in range(KB) for t in split(
                        xT_hi[:, k, b], xT_lo[:, k, b], wh_hi[:, 2, k], wh_lo[:, 2, k])]
                        + [(ones_h[:], bias_h[:, 0])], v_full)

            def scores(p, b):
                if not p.l1:
                    return
                if b == 0:
                    p.await_(pe, qkr_lo, 2 * KB)
                    if p.before.l1:
                        p.before.await_(pe, pt_lo, GROUP * KB)
                else:
                    p.await_(pe, pt_lo, b * KB)
                    p.await_(pe, s_ok, b * TILES)
                for c in range(KB):
                    for i in range(3):
                        a, m = ((qk_hi, qk_hi), (qk_hi, qk_lo), (qk_lo, qk_hi))[i]
                        for j in range(TILES):
                            rows = slice(HEAD * j, HEAD * (j + 1))
                            last = mm(psum[:, SC[j], c * TOK:(c + 1) * TOK], a[rows, 0, c, b], m[rows, 1, c, b],
                                      start=(i == 0), stop=(i == 2))
                            if c == KB - 1 and i == 2:
                                last.then_inc(s_full.sem, 1)

            def pt(p, b):
                if not p.l1:
                    return
                p.await_(pe, p_ok, (b + 1) * TILES)
                for c in range(KB):
                    for j in range(TILES):
                        last = transpose(psum[:, SC[c], j * TOK:(j + 1) * TOK], s[:, TILES * c + j], ident[:])
                    last.then_inc(pt_full.sem, 1)

            def pv(run, b):
                p = run.earlier() if b == 3 else run
                p.await_(pe, vr_lo, b + 1)
                run.await_bank(pe, "pv", b)
                p.await_(pe, pt_lo, (b + 1) * KB)
                dst = bank("pv", b)
                for h in range(HEADS):
                    terms = split(pT_hi[:, h], pT_lo[:, h], v_hi[:, b, h], v_lo[:, b, h])
                    for i, (a, m) in enumerate(terms):
                        last = mm(dst[:, h * VCOL:(h + 1) * VCOL], a, m, start=(i == 0), stop=(i == 2))
                last.then_inc(pv_full.sem, 1)

            def to(run, b):
                p = run.earlier() if b == 3 else run
                p.await_(pe, o_ok, b + 1)
                run.await_bank(pe, "to", b)
                of = o[:].rearrange("p h d -> p (h d)")
                turn("to", b, [of[:, k * 128:(k + 1) * 128] for k in range(KB)], to_full)

            def po(run, b):
                p = run.earlier() if b == 3 else run
                p.await_(pe, to_lo, b + 1)
                run.await_bank(pe, "po", b)
                product(bank("po", b)[:, 0:FEAT], [t for k in range(KB) for t in split(
                    oT_hi[:, k], oT_lo[:, k], wh_hi[:, 3, k], wh_lo[:, 3, k])]
                    + [(ones_h[:], bias_h[:, 1])], po_full)

            def body(p):
                if p.l0:
                    pe.wait_ge(xt_lo.sem, xt_lo.upto(p.it, KB))
                nl(p, 0, 0)
                if p.tail:
                    pv(p, 3)
                nl(p, 0, 1)
                if p.tail:
                    to(p, 3)
                nl(p, 0, 2)
                if p.tail:
                    po(p, 3)
                nl(p, 0, 3, 4, 5)
                if p.l1:
                    x1t(p)
                u(p, 0)
                hl(p, 0, 0, 1, 2, 3)
                ctx(p, 0)
                if p.l1:
                    qk(p)
                scores(p, 0)
                if p.l0:
                    th(p)
                if p.l1:
                    v(p)
                pt(p, 0)
                if p.l0:
                    p.await_(pe, th_lo, KB)
                nl(p, 1, 0)
                if p.l1:
                    pv(p, 0)
                scores(p, 1)
                nl(p, 1, 1)
                if p.l1:
                    to(p, 0)
                nl(p, 1, 2)
                if p.l1:
                    po(p, 0)
                nl(p, 1, 3, 4)
                pt(p, 1)
                nl(p, 1, 5)
                if p.l1:
                    pv(p, 1)
                scores(p, 2)
                hl(p, 1, 0)
                if p.l1:
                    to(p, 1)
                u(p, 1)
                if p.l1:
                    po(p, 1)
                hl(p, 1, 1)
                pt(p, 2)
                hl(p, 1, 2)
                if p.l1:
                    pv(p, 2)
                scores(p, 3)
                hl(p, 1, 3)
                if p.l1:
                    to(p, 2)
                ctx(p, 1)
                if p.l1:
                    po(p, 2)
                if p.nxt:
                    xt(p)
                pt(p, 3)

            def head():
                pe.wait_ge(const_ok, 4)
                xt(prologue)
                pe.wait_ge(ones_ok, 9)
                pe.wait_ge(w_lo_ok, 10)
                pe.wait_ge(b_lo, 6)

            passes(pe, body, head)


def kernel(x, adj, L0_gnn_W_left, L0_gnn_W_right, L0_gnn_W_lin, L0_gnn_b_lin, L0_gnn_ln_a, L0_gnn_ln_b,
           L1_gnn_Wq, L1_gnn_Wk, L1_gnn_Wv, L1_gnn_bv, L1_gnn_Wo, L1_gnn_bo):
    import numpy as np
    import concourse.bacc as bacc
    from concourse.bass_utils import run_bass_kernel_spmd

    def rows(w):
        return np.asarray(w).reshape(KB, 128, FEAT).transpose(1, 0, 2)

    per_layer = [(L0_gnn_W_left[l], L0_gnn_W_right[l], np.asarray(L0_gnn_W_lin[l]).T) for l in range(2)]
    l1 = [np.asarray(w).T for w in (L1_gnn_Wq, L1_gnn_Wk, L1_gnn_Wv, L1_gnn_Wo)]
    a, b = np.asarray(L0_gnn_ln_a), np.asarray(L0_gnn_ln_b)
    arrays = {
        "x": np.asarray(x),
        "adj": np.asarray(adj),
        "weights": np.stack([rows(w) for w in (*per_layer[0], *per_layer[1], *l1)]),
        "biases": np.stack([np.asarray(v) for v in (L0_gnn_b_lin[0], L0_gnn_b_lin[1], L1_gnn_bv, L1_gnn_bo)]),
        "ln_cols": np.ascontiguousarray(np.stack([a[0].reshape(KB, 128), b[0].reshape(KB, 128)]).transpose(2, 0, 1)),
        "ln_rows": np.stack([a[1], b[1]]),
    }
    nc = bacc.Bacc("TRN2", target_bir_lowering=False, num_devices=1, dynamic_dma_scratch_size=1024)
    args = [nc.dram_tensor(n, v.shape, mybir.dt.from_np(v.dtype), kind="ExternalInput").ap()
            for n, v in arrays.items()]
    out = nc.dram_tensor("out", (GRAPHS, TOK, FEAT), mybir.dt.float32, kind="ExternalOutput").ap()
    program(nc, *args, out)
    return run_bass_kernel_spmd(nc, [arrays], core_ids=[0]).results[0]["out"]
```

```python
import concourse.bass as bass
from concourse import mybir
from contextlib import ExitStack

GRAPHS, TOK, FEAT = 128, 128, 384
GROUP = 4
GROUPS = GRAPHS // GROUP
KB = FEAT // 128
HEADS = 12
HEAD = FEAT // HEADS
TILES = 128 // HEAD
GT = GROUP * TOK
VCOL = HEAD + 1
HCOL = FEAT + 2
TEMPER = float(FEAT) ** 0.5
WSCALE = 64.0
BIG = 3.0e38


class Signal:

    def __init__(self, sem, per_group):
        self.sem, self.per_group = sem, per_group

    def upto(self, group, n):
        return group * self.per_group + n


def program(nc, x, adj, weights, biases, ln_cols, ln_rows, out):
    f32, f32r, f16 = mybir.dt.float32, mybir.dt.float32r, mybir.dt.float16
    i32 = mybir.dt.int32
    ALU, ACT, AX = mybir.AluOpType, mybir.ActivationFunctionType, mybir.AxisListType
    mm, transpose = nc.tensor.matmul, nc.tensor.transpose

    with ExitStack() as stack:
        def sb(name, shape, dt=f32):
            return stack.enter_context(nc.sbuf_tensor(name, [128] + shape, dt))

        def sem(name):
            return stack.enter_context(nc.semaphore(name))

        ident = sb("ident", [128])
        keep_left = sb("keep_left", [TOK])
        keep_right = sb("keep_right", [TOK])
        ones_r = sb("ones_r", [128], f32r)
        ones_h = sb("ones_h", [128], f16)
        pw = sb("pw", [2, GROUP])
        wr_hi, wr_lo = (sb(f"wr_{p}", [6, KB, FEAT], f32r) for p in ("hi", "lo"))
        wh_hi, wh_lo = (sb(f"wh_{p}", [4, KB, FEAT], f16) for p in ("hi", "lo"))
        bias_r = sb("bias_r", [FEAT], f32r)
        bias_h = sb("bias_h", [FEAT], f16)
        lncol = sb("lncol", [2, KB])
        lnrow = sb("lnrow", [2, FEAT])
        xin = sb("xin", [GROUP, FEAT])
        xres = sb("xres", [GROUP, FEAT])
        adjn = sb("adjn", [GROUP, TOK])
        adjT = sb("adjT", [GROUP, TOK])
        mask = sb("mask", [GROUP, 2, TOK])
        hT_hi, hT_lo = (sb(f"hT_{p}", [KB, GROUP, TOK], f32r) for p in ("hi", "lo"))
        nT_hi, nT_lo = (sb(f"nT_{p}", [KB, 2, GROUP, TOK], f32r) for p in ("hi", "lo"))
        hl_hi, hl_lo = (sb(f"hl_{p}", [GROUP, HCOL], f32r) for p in ("hi", "lo"))
        uLR = sb("uLR", [2, 2, TOK])
        e = sb("e", [GROUP, TOK])
        hT = [e[:], uLR[:].rearrange("p b r t -> p (b r) t")]
        e_hi, e_lo = (sb(f"e_{p}", [GROUP, TOK], f32r) for p in ("hi", "lo"))
        z = sb("z", [GROUP, FEAT])
        x1 = sb("x1", [GROUP, FEAT])
        eps_den, rden = sb("eps_den", [GROUP]), sb("rden", [GROUP])
        st, mv = sb("st", [GROUP, 6]), sb("mv", [GROUP, 2])
        yst, ymv = sb("yst", [GROUP, 6]), sb("ymv", [GROUP, 2])
        yvar, yrstd, ynmr = sb("yvar", [GROUP]), sb("yrstd", [GROUP]), sb("ynmr", [GROUP])
        var, rstd, nmr = sb("var", [GROUP]), sb("rstd", [GROUP]), sb("nmr", [GROUP])
        sd = sb("sd", [GROUP])
        adj2 = sb("adj2", [GROUP, TOK])
        xT_hi, xT_lo = (sb(f"xT_{p}", [KB, GROUP, TOK], f16) for p in ("hi", "lo"))
        qk_hi, qk_lo = (sb(f"qk_{p}", [2, KB, GROUP, TOK], f16) for p in ("hi", "lo"))
        v_hi, v_lo = (sb(f"v_{p}", [GROUP, HEADS, VCOL], f16) for p in ("hi", "lo"))
        s = sb("s", [HEADS, TOK])
        w = sb("w", [HEADS, TOK])
        fold = sb("fold", [HEADS, TOK // 2])
        nmax, total, live = sb("nmax", [HEADS]), sb("total", [HEADS]), sb("live", [2, HEADS])
        pT_hi, pT_lo = (sb(f"pT_{p}", [HEADS, TOK], f16) for p in ("hi", "lo"))
        rs = sb("rs", [2, HEADS])
        o = sb("o", [HEADS, HEAD])
        oT_hi, oT_lo = (sb(f"oT_{p}", [KB, TOK], f16) for p in ("hi", "lo"))
        y2 = sb("y2", [2, FEAT])
        st2, mv2 = sb("st2", [6]), sb("mv2", [2, 2])
        var2, rstd2, nmr2 = sb("var2", [1]), sb("rstd2", [2]), sb("nmr2", [2])

        psum = stack.enter_context(nc.psum_tensor("psum", [128, 8, 512], f32))
        PJ, MX, SC = (0, 1), (2, 3), (4, 5, 6, 7)

        def signal(name, per_group):
            return Signal(sem(name), per_group)

        x_in, adj_in, xres_in = signal("x_in", 16), signal("adj_in", 16), signal("xres_in", 16)
        adj2_in = signal("adj2_in", 16)
        out_st = [signal(f"out_st{i}", 32) for i in range(2)]
        xt_full, xt_hi, xt_lo = (signal(f"xt_{p}", KB) for p in ("full", "hi", "lo"))
        adjT_full, adjT_ok, mask_ok = signal("adjT_full", 1), signal("adjT_ok", 1), signal("mask_ok", 2)
        nl_full, nl_hi, nl_lo = ([signal(f"nl{l}_{p}", 2 * KB) for l in range(2)] for p in ("full", "hi", "lo"))
        hl_full, hlr_hi, hlr_lo = ([signal(f"hl{l}_{p}", GROUP) for l in range(2)] for p in ("full", "hi", "lo"))
        u_full, u_read, u_sum, e_raw, e_ok, e_hi_ok, e_lo_ok = (
            [signal(f"{p}{l}", 2) for l in range(2)]
            for p in ("u_full", "u_read", "u_sum", "e_raw", "e_ok", "e_hi_ok", "e_lo_ok"))
        c_full, z_ok, st_ok, mv_ok = (
            [signal(f"{p}{l}", GROUP) for l in range(2)] for p in ("c_full", "z_ok", "st_ok", "mv_ok"))
        den_ok, rden_ok = ([signal(f"{p}{l}", 2) for l in range(2)] for p in ("den_ok", "rden_ok"))
        var_ok, pow_ok, eps_ok, rstd_ok = (
            [signal(f"{p}{l}", 1) for l in range(2)] for p in ("var_ok", "pow_ok", "eps_ok", "rstd_ok"))
        nmr_ok, n_ok = signal("nmr_ok", 1), signal("n_ok", GROUP)
        th_full, th_raw, th_hi, th_lo = (signal(f"th_{p}", KB) for p in ("full", "raw", "hi", "lo"))
        za_ok, zb_ok, y_ok, yst_ok, ymv_ok = (
            signal(p, GROUP) for p in ("za_ok", "zb_ok", "y_ok", "yst_ok", "ymv_ok"))
        x1_ok, x1_half = signal("x1_ok", 2), signal("x1_half", 2)
        yvar_ok, ypow_ok, ynmr_ok = (signal(p, 1) for p in ("yvar_ok", "ypow_ok", "ynmr_ok"))
        x1t_full, x1t_hi, x1t_lo = (signal(f"x1t_{p}", KB) for p in ("full", "hi", "lo"))
        qk_full, qkr_hi, qkr_lo = (signal(f"qk_{p}", 2 * KB) for p in ("full", "hi", "lo"))
        v_full, vr_hi, vr_lo = (signal(f"v_{p}", GROUP) for p in ("full", "hi", "lo"))
        adj2_ok = signal("adj2_ok", 1)
        s_full, s_ok, p_ok = (signal(p, GROUP * TILES) for p in ("s_full", "s_ok", "p_ok"))
        fold1, fold2, fold3, s_tot = (signal(p, GROUP) for p in ("fold1", "fold2", "fold3", "s_tot"))
        pt_full, pt_hi, pt_lo = (signal(f"pt_{p}", GROUP * TILES) for p in ("full", "hi", "lo"))
        pv_full, live1, live2, rs1, rs2, o_ok = (
            signal(p, GROUP) for p in ("pv_full", "live1", "live2", "rs1", "rs2", "o_ok"))
        to_full, to_hi, to_lo = (signal(f"to_{p}", GROUP) for p in ("full", "hi", "lo"))
        po_full, y2_ok, y2st_ok, y2mv_ok, y2var_ok, y2pow_ok, y2nmr_ok, fin_ok = (
            signal(p, GROUP) for p in ("po_full", "y2_ok", "y2st_ok", "y2mv_ok", "y2var_ok", "y2pow_ok",
                                       "y2nmr_ok", "fin_ok"))
        ld, w_hi_ok, w_lo_ok, const_ok, ones_ok, b_ok, b_lo = (
            sem(p) for p in ("ld", "w_hi_ok", "w_lo_ok", "const_ok", "ones_ok", "b_ok", "b_lo"))
        w_in = [sem(f"w_in{i}") for i in range(3)]

        OF_BEFORE = (adj2_in, *out_st, za_ok, zb_ok, y_ok, yst_ok, ymv_ok, x1_ok, x1_half, yvar_ok, ypow_ok,
                     ynmr_ok, x1t_full, x1t_hi, x1t_lo, qk_full, qkr_hi, qkr_lo, v_full, vr_hi, vr_lo, adj2_ok,
                     s_full, s_ok, s_tot, fold1, fold2, fold3, p_ok, pt_full, pt_hi, pt_lo, pv_full, live1, live2,
                     rs1, rs2, mv_ok[1], var_ok[1], pow_ok[1], eps_ok[1], rstd_ok[1], o_ok, to_full, to_hi, to_lo,
                     po_full, y2_ok, y2st_ok, y2mv_ok, y2var_ok, y2pow_ok, y2nmr_ok, fin_ok)
        OF_NEXT = (xt_full, xt_hi, xt_lo, adjT_full, adjT_ok)

        def ring(banks, *runs):
            stages = [(name, i, read) for name, parts, read in runs for i in parts]
            return [(name, i, banks[n % len(banks)], read) for n, (name, i, read) in enumerate(stages)]

        USES = (
            ring(PJ[::-1] + SC[:2], ("nl0", range(6), nl_lo[0]))
            + ring(SC[3:], ("po", (3,), y2_ok))
            + ring(SC[:2], ("hl0", (0, 1), hlr_lo[0]))
            + ring(PJ, ("hl0", (2, 3), hlr_lo[0]), ("qk", range(6), qkr_lo), ("v", range(4), vr_lo),
                       ("nl1", range(5), nl_lo[1]), ("po", (0,), y2_ok), ("nl1", (5,), nl_lo[1]),
                       ("hl1", (0, 1), hlr_lo[1]), ("po", (1,), y2_ok), ("hl1", (2, 3), hlr_lo[1]),
                       ("xt", (2,), xt_lo), ("adjT", (0,), adjT_ok), ("po", (2,), y2_ok))
            + ring(MX[::-1], ("pv", (3,), o_ok), ("to", (3,), to_lo), ("u0", (0, 1), u_read[0]),
                             ("th", range(3), th_hi), ("pt", range(4), pt_lo), ("pv", (0,), o_ok),
                             ("pt", range(4, 8), pt_lo), ("to", (0,), to_lo), ("pv", (1,), o_ok),
                             ("pt", range(8, 11), pt_lo), ("to", (1,), to_lo), ("pt", (11,), pt_lo),
                             ("u1", (0,), u_read[1]), ("pv", (2,), o_ok), ("u1", (1,), u_read[1]),
                             ("to", (2,), to_lo))
            + ring(MX, ("xt", range(2), xt_lo))
            + ring((SC[2], SC[3], SC[0]), ("x1t", range(3), x1t_lo))
            + ring(SC, ("c0", range(4), z_ok[0]))
            + ring(SC, ("s", range(12, 16), s_ok))
            + ring(SC, ("pt", range(12, 16), pt_lo))
            + ring(SC, ("c1", range(4), z_ok[1])))
        TAIL = (("pv", 3), ("to", 3), ("po", 3))
        L1_STAGES = ("x1t", "qk", "v", "s", "pt", "pv", "to", "po")
        NEXT_STAGES = ("xt", "adjT")

        def place(stage, i):
            b, = (use[2] for use in USES if use[:2] == (stage, i))
            order = [use for use in USES if use[2] == b]
            return b, order, [use[:2] for use in order].index((stage, i))

        def bank(stage, i):
            return psum[:, place(stage, i)[0], :]

        class Pass:

            def __init__(self, it, l0=True, l1=True, nxt=True, tail=True, before=None,
                         setup=False):
                self.it, self.l0, self.l1, self.nxt, self.tail, self.before = it, l0, l1, nxt, tail, before
                self.setup = setup

            def has(self, use):
                if use in TAIL:
                    return self.tail
                return self.l1 if use[0] in L1_STAGES else self.nxt if use[0] in NEXT_STAGES else self.l0

            def group(self, sig):
                return self.it - 1 if sig in OF_BEFORE else self.it + 1 if sig in OF_NEXT else self.it

            def earlier(self):
                return Pass(self.it - 1)

            def await_(self, eng, sig, n):
                eng.wait_ge(sig.sem, sig.upto(self.group(sig), n))

            def await_apart(self, eng, sig, n):
                value = sig.upto(self.group(sig), n)
                if not isinstance(value, int):
                    value = eng.snap(eng.to_reg(value), min_val=1)
                eng.wait_ge(sig.sem, 1)
                eng.wait_ge(sig.sem, value)

            def await_bank(self, eng, stage, i):
                _, order, n = place(stage, i)
                candidates = [(self, m) for m in range(n - 1, -1, -1)]
                if self.before:
                    candidates += [(self.before, m) for m in range(len(order) - 1, -1, -1)]
                for run, m in candidates:
                    name, j, _, read = order[m]
                    if run.has((name, j)):
                        group = run.group(read) - (1 if (name, j) in TAIL else 0)
                        eng.wait_ge(read.sem, read.upto(group, j + 1))
                        return

        def passes(eng, body, head=None):
            if head:
                head()
            first = Pass(0, l1=False, tail=False, before=prologue, setup=True)
            body(first)
            body(Pass(1, tail=False, before=first))
            with eng.Fori(2, GROUPS - 1) as it:
                body(Pass(it, before=Pass(it - 1)))
            body(Pass(GROUPS - 1, nxt=False, before=Pass(GROUPS - 2)))
            body(Pass(GROUPS, l0=False, nxt=False, before=Pass(GROUPS - 1, nxt=False)))
            body(Pass(GROUPS + 1, l0=False, l1=False, nxt=False, before=Pass(GROUPS, l0=False, nxt=False)))

        prologue = Pass(-1, l0=False, l1=False, tail=False)

        stage_w = [x1[:, 0:KB]] + [b[:].rearrange("p h t -> p (h t)")[:, 0:KB * FEAT].rearrange(
            "p (k f) -> p k f", k=KB) for b in (s, w)]
        stage_b = fold[:].rearrange("p (a h) t -> p a (h t)", a=2)

        block = stack.enter_context(nc.Block())

        @block.sync
        def _(sp):
            sp.dma_start(xin[:], x[0:GROUP].rearrange("b t f -> t b f")).then_inc(x_in.sem, 16)
            for m in range(10):
                if m >= 3:
                    sp.wait_ge(w_lo_ok, m - 2)
                sp.dma_start(stage_w[m % 3], weights[m]).then_inc(w_in[m % 3], 16)
                if m == 1:
                    sp.dma_start(adjn[:], adj[0:GROUP].rearrange("b i j -> i b j")).then_inc(adj_in.sem, 16)
                if m == 2:
                    sp.wait_ge(const_ok, 1)
                    for row in range(0, 128, 32):
                        pair = biases[row // 64::2]
                        sp.dma_start(stage_b[row:row + 1, :, :], pair[None, :, :]).then_inc(ld, 16)
                    sp.dma_start(lncol[:], ln_cols).then_inc(ld, 16)
                    sp.dma_start(lnrow[:], ln_rows.rearrange("a f -> (a f)")[None, :].to_broadcast([128, 2 * FEAT]))\
                        .then_inc(ld, 16)

            def store(p, b):
                p.await_(sp, fin_ok, b + 1)
                sp.dma_start(out[bass.ds((p.it - 1) * GROUP + b, 1)].rearrange("b t f -> t (b f)"), y2[:, b % 2])\
                    .then_inc(out_st[b % 2].sem, 16)

            def body(p):
                it = p.it
                if p.l1:
                    if p.before.l1:
                        p.before.await_(sp, s_ok, GROUP * TILES)
                    sp.dma_start(adj2[:], adj[bass.ds((it - 1) * GROUP, GROUP)].rearrange("b i j -> i b j"))\
                        .then_inc(adj2_in.sem, 16)
                if p.nxt:
                    sp.wait_ge(xt_full.sem, xt_full.upto(it, KB))
                    sp.dma_start(xin[:], x[bass.ds((it + 1) * GROUP, GROUP)].rearrange("b t f -> t b f"))\
                        .then_inc(x_in.sem, 16)
                    sp.wait_ge(adjT_full.sem, adjT_full.upto(it, 1))
                    sp.wait_ge(mask_ok.sem, mask_ok.upto(it, 2))
                    sp.dma_start(adjn[:], adj[bass.ds((it + 1) * GROUP, GROUP)].rearrange("b i j -> i b j"))\
                        .then_inc(adj_in.sem, 16)
                if p.tail:
                    store(p.earlier(), 3)
                if p.l0:
                    if p.l1:
                        p.await_(sp, y_ok, GROUP)
                    sp.dma_start(xres[:], x[bass.ds(it * GROUP, GROUP)].rearrange("b t f -> t b f"))\
                        .then_inc(xres_in.sem, 16)
                if p.l1:
                    for b in range(3):
                        store(p, b)

            passes(sp, body)
            for i in range(2):
                sp.wait_ge(out_st[i].sem, out_st[i].upto(GROUPS - 1, 32))

        @block.gpsimd
        def _(pool):
            nc.gpsimd.memset(stage_b[:], 0.0).then_inc(const_ok, 1)
            nc.gpsimd.memset(ident[:], 0.0).then_inc(b_ok, 1)
            nc.gpsimd.memset(keep_left[:], 1.0 / TEMPER).then_inc(b_ok, 1)
            nc.gpsimd.memset(keep_right[:], 1.0 / TEMPER).then_inc(b_ok, 1)
            nc.gpsimd.memset(pw[:, 0], 0.5).then_inc(ones_ok, 1)
            nc.gpsimd.memset(pw[:, 1], -0.5).then_inc(ones_ok, 1)
            nc.gpsimd.memset(ones_r[:].bitcast(f32), 1.0).then_inc(ones_ok, 1)
            nc.gpsimd.memset(ones_h[:], 1.0).then_inc(ones_ok, 1)
            nc.gpsimd.memset(hl_hi[:, :, FEAT:FEAT + 1].bitcast(f32), 1.0).then_inc(ones_ok, 1)
            nc.gpsimd.memset(hl_hi[:, :, FEAT + 1:HCOL].bitcast(f32), 0.0).then_inc(ones_ok, 1)
            nc.gpsimd.memset(hl_lo[:, :, FEAT:HCOL].bitcast(f32), 0.0).then_inc(ones_ok, 1)
            nc.gpsimd.memset(v_hi[:, :, :, HEAD:VCOL], 1.0).then_inc(ones_ok, 1)
            nc.gpsimd.memset(v_lo[:, :, :, HEAD:VCOL], 0.0).then_inc(ones_ok, 1)
            pool.wait_ge(b_ok, 3)
            nc.gpsimd.affine_select(out=ident[:], in_=ident[:], compare_op=ALU.not_equal, fill=1.0, base=0,
                                    pattern=[[-1, 128]], channel_multiplier=1).then_inc(const_ok, 1)
            nc.gpsimd.affine_select(out=keep_left[:], in_=keep_left[:], compare_op=ALU.is_ge, fill=0.0, base=0,
                                    pattern=[[-1, TOK]], channel_multiplier=1).then_inc(const_ok, 1)
            nc.gpsimd.affine_select(out=keep_right[:], in_=keep_right[:], compare_op=ALU.is_gt, fill=0.0, base=0,
                                    pattern=[[1, TOK]], channel_multiplier=-1).then_inc(const_ok, 1)
            pool.wait_ge(const_ok, 4)
            pool.wait_ge(ones_ok, 9)

            def masks(p, sig_group):
                pool.wait_ge(adj_in.sem, adj_in.upto(sig_group, 16))
                pool.wait_ge(adjT_ok.sem, adjT_ok.upto(sig_group, 1))
                if p is not None:
                    p.await_(pool, u_read[1], 2)
                nc.gpsimd.tensor_tensor(mask[:, :, 0], adjT[:], keep_L, ALU.mult).then_inc(mask_ok.sem, 1)
                nc.gpsimd.tensor_tensor(mask[:, :, 1], adjn[:], keep_R, ALU.mult).then_inc(mask_ok.sem, 1)

            keep_L = keep_left[:, None, :].to_broadcast([128, GROUP, TOK])
            keep_R = keep_right[:, None, :].to_broadcast([128, GROUP, TOK])

            def weigh(p, l):
                for h in range(2):
                    part = slice(2 * h, 2 * h + 2)
                    p.await_(pool, e_raw[l], h + 1)
                    nc.gpsimd.tensor_tensor(e[:, part], e[:, part], adjT[:, part], ALU.mult).then_inc(e_ok[l].sem, 1)
                for h in range(2):
                    part = slice(2 * h, 2 * h + 2)
                    p.await_(pool, e_hi_ok[l], h + 1)
                    p.await_(pool, e_ok[l], h + 1)
                    nc.gpsimd.tensor_tensor(e_lo[:, part], e[:, part], e_hi[:, part].bitcast(f32), ALU.subtract)\
                        .then_inc(e_lo_ok[l].sem, 1)

            def power(p, src_ok, dst, src, exponent, done, n=1):
                p.await_(pool, src_ok, n)
                w = dst.shape[-1]
                nc.gpsimd.tensor_tensor(dst, src, pw[:, exponent, 0:w], ALU.pow).then_inc(done.sem, 1)

            def folds(p, b):
                if not p.l1:
                    return
                p.await_(pool, s_ok, (b + 1) * TILES)
                if b > 0:
                    p.await_(pool, s_tot, b)
                elif p.before.l1:
                    p.before.await_(pool, s_tot, GROUP)
                src = s[:]
                for n, done in ((TOK // 2, fold1), (TOK // 4, fold2), (TOK // 8, fold3)):
                    if n < TOK // 2:
                        p.await_(pool, fold1 if n == TOK // 4 else fold2, b + 1)
                    nc.gpsimd.tensor_tensor(fold[:, :, 0:n], src[:, :, 0:n], src[:, :, n:2 * n], ALU.add)\
                        .then_inc(done.sem, 1)
                    src = fold[:]

            def y2_power(p, b):
                power(p, y2var_ok, rstd2[:, b % 2:b % 2 + 1], var2[:], 1, y2pow_ok, b + 1)

            def body(p):
                if p.l1:
                    power(p, var_ok[1], sd[:], var[:], 0, pow_ok[1])
                    power(p, yvar_ok, yrstd[:], yvar[:], 1, ypow_ok)
                    p.await_apart(pool, adj2_in, 16)
                if p.tail:
                    y2_power(p.earlier(), 3)
                if p.l1:
                    nc.gpsimd.tensor_scalar(adj2[:], adj2[:], 2.0, TEMPER, ALU.mult, ALU.mult)\
                        .then_inc(adj2_ok.sem, 1)
                if p.l0:
                    weigh(p, 0)
                    power(p, var_ok[0], sd[:], var[:], 0, pow_ok[0])
                folds(p, 0)
                folds(p, 1)
                folds(p, 2)
                if p.l1:
                    y2_power(p, 0)
                folds(p, 3)
                if p.l1:
                    y2_power(p, 1)
                if p.l0:
                    weigh(p, 1)
                if p.nxt:
                    masks(p, p.it + 1)
                if p.l1:
                    y2_power(p, 2)

            def head():
                masks(None, 0)

            passes(pool, body, head)

        @block.scalar
        def _(act):
            def copy(dst, src, scale=1.0):
                return nc.scalar.activation(dst, src, ACT.Copy, scale=scale)

            def weight(m):
                act.wait_ge(w_in[m % 3], 16 * (m // 3 + 1))
                if m < 6:
                    copy(wr_hi[:, m], stage_w[m % 3]).then_inc(w_hi_ok, 1)
                else:
                    copy(wh_hi[:, m - 6], stage_w[m % 3], WSCALE).then_inc(w_hi_ok, 1)

            def hi(p, full, n, stage, dst, done, scale=1.0):
                p.await_(act, full, n + 1)
                w = 1
                for d in dst.shape[1:]:
                    w *= d
                src = bank(stage, n)[:, 0:w]
                if len(dst.shape) == 3:
                    src = src.rearrange("p (a b) -> p a b", a=dst.shape[1])
                copy(dst, src, scale).then_inc(done.sem, 1)

            def xt(p):
                for k in range(KB):
                    hi(p, xt_full, k, "xt", hT_hi[:, k], xt_hi)
                p.await_(act, adjT_full, 1)
                if p.l0:
                    p.await_(act, e_ok[1], 2)
                copy(adjT[:], bank("adjT", 0).rearrange("p (a b) -> p a b", a=GROUP)).then_inc(adjT_ok.sem, 1)

            def nl(p, l, c):
                if p.l0:
                    lr, kb = divmod(c, KB)
                    hi(p, nl_full[l], c, f"nl{l}", nT_hi[:, kb, lr], nl_hi[l])

            def hl(p, l, b):
                if p.l0:
                    hi(p, hl_full[l], b, f"hl{l}", hl_hi[:, b, 0:FEAT], hlr_hi[l])

            def v(p, b):
                p.await_(act, v_full, b + 1)
                copy(v_hi[:, b, :, 0:HEAD], bank("v", b)[:, 0:FEAT].rearrange("p (h d) -> p h d", h=HEADS),
                     1.0 / WSCALE).then_inc(vr_hi.sem, 1)

            def exps(p, b, j):
                if not p.l1:
                    return
                p.await_(act, s_ok, b * TILES + j + 1)
                for c in range(KB):
                    h = TILES * c + j
                    last = nc.scalar.activation(w[:, h], s[:, h], ACT.Exp, bias=nmax[:, h:h + 1], scale=-1.0)
                last.then_inc(p_ok.sem, 1)

            def exp_u(p, l, h):
                if p.l0:
                    p.await_(act, u_sum[l], h + 1)
                    nc.scalar.activation(e[:, 2 * h:2 * h + 2], e[:, 2 * h:2 * h + 2], ACT.Exp).then_inc(e_raw[l].sem, 1)

            def round_e(p, l, h):
                if p.l0:
                    p.await_(act, e_ok[l], h + 1)
                    copy(e_hi[:, 2 * h:2 * h + 2], e[:, 2 * h:2 * h + 2]).then_inc(e_hi_ok[l].sem, 1)

            def pt(p, b, *js):
                for j in js if p.l1 else ():
                    n = b * TILES + j
                    p.await_(act, pt_full, n + 1)
                    copy(pT_hi[:, j::TILES], bank("pt", n)[:, 0:KB * TOK].rearrange("p (a b) -> p a b", a=KB))\
                        .then_inc(pt_hi.sem, 1)

            def ctx(p, l, b):
                if p.l0:
                    p.await_(act, rden_ok[l], b // 2 + 1)
                    copy(z[:, b], bank(f"c{l}", b)[:, 0:FEAT], scale=rden[:, b:b + 1]).then_inc(z_ok[l].sem, 1)

            def th(p, k):
                if not p.l0:
                    return
                if p.setup and k == 0:
                    act.wait_ge(ld, 96)
                p.await_(act, th_full, k + 1)
                src = bank("th", k).rearrange("p (a b) -> p a b", a=GROUP)
                if k == 2:
                    p.await_(act, th_lo, 1)
                for dst, done in ((hT[k % 2], th_raw), (hT_hi[:, k], th_hi)):
                    nc.scalar.activation(dst, src, ACT.Relu, bias=lncol[:, 1, k:k + 1], scale=lncol[:, 0, k:k + 1])\
                        .then_inc(done.sem, 1)

            def to(p, b):
                hi(p, to_full, b, "to", oT_hi[:], to_hi)

            def fin(p, b):
                p.await_(act, y2nmr_ok, b + 1)
                nc.scalar.activation(y2[:, b % 2], y2[:, b % 2], ACT.Identity,
                                     bias=nmr2[:, b % 2:b % 2 + 1], scale=rstd2[:, b % 2:b % 2 + 1])\
                    .then_inc(fin_ok.sem, 1)

            def x1t(p):
                for k in range(KB):
                    hi(p, x1t_full, k, "x1t", xT_hi[:, k], x1t_hi)

            def x1_norm(p, *bs):
                p.await_(act, ynmr_ok, 1)
                for b in bs:
                    nc.scalar.activation(x1[:, b], x1[:, b], ACT.Identity,
                                         bias=ynmr[:, b:b + 1], scale=yrstd[:, b:b + 1]).then_inc(x1_half.sem, 1)

            def qk(p, *cs):
                for c in cs if p.l1 else ():
                    hi(p, qk_full, c, "qk", qk_hi[:, c // KB, c % KB], qkr_hi, 1.0 / WSCALE)

            def body(p):
                nl(p, 0, 0)
                if p.setup:
                    weight(2)
                nl(p, 0, 1)
                if p.setup:
                    weight(3)
                nl(p, 0, 2)
                if p.tail:
                    to(p.earlier(), 3)
                nl(p, 0, 3)
                if p.tail:
                    fin(p.earlier(), 2)
                nl(p, 0, 4)
                nl(p, 0, 5)
                hl(p, 0, 0)
                if p.l1:
                    x1_norm(p, 2, 3)
                if p.setup:
                    weight(4)
                    weight(5)
                hl(p, 0, 1)
                if p.l1:
                    x1t(p)
                exp_u(p, 0, 0)
                if p.tail:
                    fin(p.earlier(), 3)
                hl(p, 0, 2)
                exp_u(p, 0, 1)
                round_e(p, 0, 0)
                hl(p, 0, 3)
                qk(p, 0, 1)
                round_e(p, 0, 1)
                qk(p, 2)
                for b in range(GROUP):
                    ctx(p, 0, b)
                qk(p, 3, 4, 5)
                if p.l1:
                    v(p, 0)
                exps(p, 0, 0)
                if p.l1:
                    v(p, 1)
                    v(p, 2)
                th(p, 0)
                th(p, 1)
                exps(p, 0, 1)
                th(p, 2)
                if p.l1:
                    v(p, 3)
                if p.setup:
                    weight(6)
                exps(p, 0, 2)
                pt(p, 0, 0)
                exps(p, 0, 3)
                pt(p, 0, 1)
                nl(p, 1, 0)
                pt(p, 0, 2)
                exps(p, 1, 0)
                pt(p, 0, 3)
                exps(p, 1, 1)
                exps(p, 1, 2)
                nl(p, 1, 1)
                exps(p, 1, 3)
                if p.setup:
                    weight(7)
                nl(p, 1, 2)
                pt(p, 1, 0, 1)
                nl(p, 1, 3)
                if p.setup:
                    weight(8)
                pt(p, 1, 2, 3)
                if p.l1:
                    to(p, 0)
                nl(p, 1, 4)
                exps(p, 2, 0)
                exps(p, 2, 1)
                exps(p, 2, 2)
                exps(p, 2, 3)
                pt(p, 2, 0)
                nl(p, 1, 5)
                if p.setup:
                    weight(9)
                hl(p, 1, 0)
                pt(p, 2, 1, 2)
                if p.l1:
                    to(p, 1)
                pt(p, 2, 3)
                exps(p, 3, 0)
                hl(p, 1, 1)
                exp_u(p, 1, 0)
                exps(p, 3, 1)
                exps(p, 3, 2)
                if p.l1:
                    fin(p, 0)
                exps(p, 3, 3)
                pt(p, 3, 0)
                if p.l1:
                    to(p, 2)
                exp_u(p, 1, 1)
                pt(p, 3, 1)
                round_e(p, 1, 0)
                pt(p, 3, 2)
                hl(p, 1, 2)
                round_e(p, 1, 1)
                hl(p, 1, 3)
                pt(p, 3, 3)
                if p.nxt:
                    xt(p)
                if p.l1:
                    fin(p, 1)
                for b in range(GROUP):
                    ctx(p, 1, b)

            def head():
                weight(0)
                weight(1)
                xt(prologue)

            passes(act, body, head)

        @block.vector
        def _(dve):
            def weight(m):
                dve.wait_ge(w_hi_ok, m + 1)
                if m < 6:
                    nc.vector.tensor_tensor(wr_lo[:, m], stage_w[m % 3], wr_hi[:, m].bitcast(f32), ALU.subtract)\
                        .then_inc(w_lo_ok, 1)
                else:
                    nc.vector.scalar_tensor_tensor(wh_lo[:, m - 6], stage_w[m % 3], WSCALE, wh_hi[:, m - 6],
                                                   ALU.mult, ALU.subtract).then_inc(w_lo_ok, 1)

            def split_biases():
                dve.wait_ge(ld, 96)
                nc.vector.tensor_copy(bias_r[:], stage_b[:, 0]).then_inc(b_lo, 1)
                nc.vector.tensor_scalar(bias_h[:], stage_b[:, 1], WSCALE, None, ALU.mult).then_inc(b_lo, 1)
                dve.wait_ge(b_lo, 2)
                for n, first in enumerate((32, 96)):
                    rows = slice(first, first + 32)
                    nc.vector.tensor_tensor(stage_b[rows, 0], stage_b[rows, 0], bias_r[rows].bitcast(f32), ALU.subtract)\
                        .then_inc(b_lo, 1)
                    nc.vector.scalar_tensor_tensor(stage_b[rows, 1], stage_b[rows, 1], WSCALE, bias_h[rows],
                                                   ALU.mult, ALU.subtract).then_inc(b_lo, 1)
                    dve.wait_ge(b_lo, 4 * n + 4)
                    nc.vector.tensor_copy(bias_r[rows], stage_b[rows, 0]).then_inc(b_lo, 1)
                    nc.vector.tensor_copy(bias_h[rows], stage_b[rows, 1]).then_inc(b_lo, 1)
                dve.wait_ge(b_lo, 10)

            def lo(p, hi_ok, n, stage, dst, rounded, done, scale=None):
                p.await_(dve, hi_ok, n + 1)
                w = 1
                for d in dst.shape[1:]:
                    w *= d
                src = bank(stage, n)[:, 0:w]
                if len(dst.shape) == 3:
                    src = src.rearrange("p (a b) -> p a b", a=dst.shape[1])
                if scale is None:
                    nc.vector.tensor_tensor(dst, src, rounded, ALU.subtract).then_inc(done.sem, 1)
                else:
                    nc.vector.scalar_tensor_tensor(dst, src, scale, rounded, ALU.mult, ALU.subtract)\
                        .then_inc(done.sem, 1)

            def xt(p):
                for k in range(KB):
                    lo(p, xt_hi, k, "xt", hT_lo[:, k], hT_hi[:, k].bitcast(f32), xt_lo)

            def nl(p, l, *cs):
                for c in cs if p.l0 else ():
                    lr, kb = divmod(c, KB)
                    lo(p, nl_hi[l], c, f"nl{l}", nT_lo[:, kb, lr], nT_hi[:, kb, lr].bitcast(f32), nl_lo[l])

            def hl(p, l, b):
                if p.l0:
                    lo(p, hlr_hi[l], b, f"hl{l}", hl_lo[:, b, 0:FEAT], hl_hi[:, b, 0:FEAT].bitcast(f32), hlr_lo[l])

            def scores(p, b, j):
                if not p.l1:
                    return
                if b == 0 and j == 0:
                    p.await_apart(dve, adj2_ok, 1)
                if b > 0:
                    if j == 0:
                        p.await_apart(dve, live1, b)
                        p.await_apart(dve, fold1, b)
                    p.await_apart(dve, p_ok, (b - 1) * TILES + j + 1)
                elif j == 0 and p.before.l1:
                    p.before.await_apart(dve, fold1, GROUP)
                p.await_apart(dve, s_full, b * TILES + j + 1)
                for c in range(KB):
                    h = TILES * c + j
                    last = nc.vector.tensor_tensor_reduce(
                        out=s[:, h], in0=psum[:, SC[j], c * TOK:(c + 1) * TOK], in1=adj2[:, b],
                        scale=-1.0 / TEMPER, scalar=BIG, op0=ALU.add, op1=ALU.min, accum_out=nmax[:, h:h + 1])
                last.then_inc(s_ok.sem, 1)

            def peaks(p, b):
                if not p.l1:
                    return
                if b > 0:
                    p.await_(dve, live2, b)
                p.await_(dve, s_ok, (b + 1) * TILES)
                nc.vector.tensor_scalar(live[:, 0], nmax[:], 0.0, None, ALU.not_equal).then_inc(live1.sem, 1)

            def guard(p, b):
                if not p.l1:
                    return
                p.await_(dve, fold3, b + 1)
                nc.vector.tensor_reduce(total[:], fold[:, :, 0:TOK // 8], AX.X, ALU.add).then_inc(s_tot.sem, 1)
                p.await_(dve, live1, b + 1)
                p.await_(dve, s_tot, b + 1)
                nc.vector.scalar_tensor_tensor(live[:, 1], total[:], 0.0, live[:, 0], ALU.not_equal, ALU.max)\
                    .then_inc(live2.sem, 1)

            def pt(p, b, *js):
                for j in js if p.l1 else ():
                    n = b * TILES + j
                    p.await_(dve, pt_hi, n + 1)
                    nc.vector.tensor_tensor(
                        pT_lo[:, j::TILES], bank("pt", n)[:, 0:KB * TOK].rearrange("p (a b) -> p a b", a=KB),
                        pT_hi[:, j::TILES], ALU.subtract).then_inc(pt_lo.sem, 1)

            def pv(p, b):
                src = bank("pv", b)[:, 0:HEADS * VCOL].rearrange("p (h d) -> p h d", h=HEADS)
                p.await_(dve, pv_full, b + 1)
                nc.vector.reciprocal(rs[:, 0], src[:, :, HEAD]).then_inc(rs1.sem, 1)
                p.await_(dve, rs1, b + 1)
                p.await_(dve, live2, b + 1)
                nc.vector.tensor_tensor(rs[:, 1], rs[:, 0], live[:, 1], ALU.mult).then_inc(rs2.sem, 1)
                p.await_(dve, rs2, b + 1)
                nc.vector.tensor_tensor(o[:], src[:, :, 0:HEAD],
                                        rs[:, 1, :, None].to_broadcast([128, HEADS, HEAD]), ALU.mult)\
                    .then_inc(o_ok.sem, 1)

            def to(p, b):
                lo(p, to_hi, b, "to", oT_lo[:], oT_hi[:], to_lo)

            def po(p, b):
                p.await_(dve, po_full, b + 1)
                if b >= 2:
                    p.await_(dve, out_st[b % 2], 16)
                elif p.tail:
                    p.before.await_(dve, out_st[b % 2], 32)
                nc.vector.scalar_tensor_tensor(y2[:, b % 2], bank("po", b)[:, 0:FEAT], 1.0 / WSCALE, x1[:, b],
                                               ALU.mult, ALU.add).then_inc(y2_ok.sem, 1)

            def po_stats(p, b):
                p.await_(dve, y2_ok, b + 1)
                nc.vector.bn_stats(st2[:], y2[:, b % 2]).then_inc(y2st_ok.sem, 1)
                p.await_apart(dve, y2st_ok, b + 1)
                nc.vector.bn_aggr(mv2[:, b % 2], st2[:]).then_inc(y2mv_ok.sem, 1)
                p.await_(dve, y2mv_ok, b + 1)
                nc.vector.tensor_scalar(var2[:], mv2[:, b % 2, 1:2], 1e-5, None, ALU.add).then_inc(y2var_ok.sem, 1)

            def fin(p, b):
                p.await_(dve, y2pow_ok, b + 1)
                nc.vector.scalar_tensor_tensor(nmr2[:, b % 2:b % 2 + 1], mv2[:, b % 2, 0:1], -1.0,
                                               rstd2[:, b % 2:b % 2 + 1], ALU.mult, ALU.mult)\
                    .then_inc(y2nmr_ok.sem, 1)

            def u(p, l, h):
                if not p.l0:
                    return
                p.await_(dve, u_full[l], h + 1)
                if h == 1:
                    p.await_(dve, u_sum[l], 1)
                if l == 0 and h == 0:
                    dve.wait_ge(mask_ok.sem, mask_ok.upto(p.it, 2))
                nc.vector.tensor_tensor(uLR[:], bank(f"u{l}", h).rearrange("p (b r t) -> p b r t", b=2, r=2),
                                        mask[:, 2 * h:2 * h + 2], ALU.mult).then_inc(u_read[l].sem, 1)
                p.await_(dve, u_read[l], h + 1)
                nc.vector.tensor_tensor(e[:, 2 * h:2 * h + 2], uLR[:, :, 0], uLR[:, :, 1], ALU.add)\
                    .then_inc(u_sum[l].sem, 1)

            def den(p, l, h):
                if not p.l0:
                    return
                two = slice(2 * h, 2 * h + 2)
                first = place(f"c{l}", 2 * h)[0]
                p.await_(dve, c_full[l], 2 * h + 2)
                nc.vector.tensor_scalar(eps_den[:, two], psum[:, first:first + 2, FEAT], 1e-10, None, ALU.add)\
                    .then_inc(den_ok[l].sem, 1)
                p.await_(dve, den_ok[l], h + 1)
                nc.vector.reciprocal(rden[:, two], eps_den[:, two]).then_inc(rden_ok[l].sem, 1)

            def bn(of, src, src_ok, st, done, *bs):
                for b in bs:
                    of.await_(dve, src_ok, b + 1)
                    nc.vector.bn_stats(st[:, b], src[:, b]).then_inc(done.sem, 1)

            def variance(p, st, mv, var, st_done, mv_done, var_done, factor, eps, of=None):
                for b in range(GROUP):
                    (of or p).await_apart(dve, st_done, b + 1)
                    nc.vector.bn_aggr(mv[:, b], st[:, b]).then_inc(mv_done.sem, 1)
                p.await_(dve, mv_done, GROUP)
                nc.vector.tensor_scalar(var[:], mv[:, :, 1], factor, eps, ALU.mult, ALU.add).then_inc(var_done.sem, 1)

            def z_variance(p, l):
                variance(p, st, mv, var, st_ok[l], mv_ok[l], var_ok[l], FEAT / (FEAT - 1.0), 0.0,
                         of=p.before if l else p)

            def inv_std(p, l):
                p.await_(dve, pow_ok[l], 1)
                nc.vector.tensor_scalar(var[:], sd[:], 1e-3, None, ALU.add).then_inc(eps_ok[l].sem, 1)
                p.await_(dve, eps_ok[l], 1)
                nc.vector.reciprocal(rstd[:], var[:]).then_inc(rstd_ok[l].sem, 1)

            def z_norm(p):
                if not p.l0:
                    return
                inv_std(p, 0)
                p.await_(dve, rstd_ok[0], 1)
                nc.vector.scalar_tensor_tensor(nmr[:], mv[:, :, 0], -1.0, rstd[:], ALU.mult, ALU.mult)\
                    .then_inc(nmr_ok.sem, 1)
                p.await_(dve, nmr_ok, 1)

            def norm_z(p, *bs):
                for b in bs if p.l0 else ():
                    nc.vector.tensor_scalar(z[:, b], z[:, b], rstd[:, b:b + 1], nmr[:, b:b + 1], ALU.mult, ALU.add)\
                        .then_inc(n_ok.sem, 1)

            def scale_z(p, *bs):
                for b in bs if p.l1 else ():
                    nc.vector.scalar_tensor_tensor(z[:, b], z[:, b], mv[:, b, 0:1], lnrow[:, 0], ALU.subtract, ALU.mult)\
                        .then_inc(za_ok.sem, 1)

            def shift_z(p, *bs):
                for b in bs if p.l1 else ():
                    if b == 0:
                        p.await_(dve, rstd_ok[1], 1)
                    p.await_(dve, za_ok, b + 1)
                    nc.vector.scalar_tensor_tensor(z[:, b], z[:, b], rstd[:, b:b + 1], lnrow[:, 1], ALU.mult, ALU.add)\
                        .then_inc(zb_ok.sem, 1)

            def th(p, k):
                p.await_(dve, th_hi, k + 1)
                nc.vector.tensor_tensor(hT_lo[:, k], hT[k % 2], hT_hi[:, k].bitcast(f32), ALU.subtract)\
                    .then_inc(th_lo.sem, 1)

            def resid(p, *bs):
                for b in bs if p.l1 else ():
                    if b == 0:
                        p.before.await_(dve, xres_in, 16)
                    if b == 3 and p.tail:
                        p.earlier().await_(dve, y2_ok, GROUP)
                    p.await_(dve, zb_ok, b + 1)
                    nc.vector.scalar_tensor_tensor(x1[:, b], z[:, b], 0.0, xres[:, b], ALU.max, ALU.add)\
                        .then_inc(y_ok.sem, 1)

            def resid_inv(p):
                p.await_(dve, ypow_ok, 1)
                nc.vector.scalar_tensor_tensor(ynmr[:], ymv[:, :, 0], -1.0, yrstd[:], ALU.mult, ALU.mult)\
                    .then_inc(ynmr_ok.sem, 1)

            def resid_norm(p, *bs):
                p.await_(dve, ynmr_ok, 1)
                for b in bs:
                    nc.vector.tensor_scalar(x1[:, b], x1[:, b], yrstd[:, b:b + 1], ynmr[:, b:b + 1], ALU.mult, ALU.add)\
                        .then_inc(x1_ok.sem, 1)

            def v(p, b):
                p.await_(dve, vr_hi, b + 1)
                nc.vector.scalar_tensor_tensor(
                    v_lo[:, b, :, 0:HEAD], bank("v", b)[:, 0:FEAT].rearrange("p (h d) -> p h d", h=HEADS),
                    1.0 / WSCALE, v_hi[:, b, :, 0:HEAD], ALU.mult, ALU.subtract).then_inc(vr_lo.sem, 1)

            def qk(p, *cs):
                for c in cs if p.l1 else ():
                    lo(p, qkr_hi, c, "qk", qk_lo[:, c // KB, c % KB], qk_hi[:, c // KB, c % KB], qkr_lo, 1.0 / WSCALE)

            def x1t(p):
                for k in range(KB):
                    lo(p, x1t_hi, k, "x1t", xT_lo[:, k], xT_hi[:, k], x1t_lo)

            def body(p):
                tail = p.earlier()
                nl(p, 0, 0)
                if p.l1:
                    z_variance(p, 1)
                if p.tail:
                    fin(tail, 2)
                    pv(tail, 3)
                if p.setup:
                    weight(2)
                scale_z(p, 0)
                if p.l1:
                    inv_std(p, 1)
                scale_z(p, 1)
                nl(p, 0, 1)
                scale_z(p, 2)
                nl(p, 0, 2)
                scale_z(p, 3)
                shift_z(p, 0)
                if p.tail:
                    to(tail, 3)
                shift_z(p, 1)
                resid(p, 0)
                nl(p, 0, 3)
                if p.setup:
                    split_biases()
                shift_z(p, 2)
                resid(p, 1)
                shift_z(p, 3)
                if p.setup:
                    weight(3)
                if p.l1:
                    bn(p, x1, y_ok, yst, yst_ok, 0)
                resid(p, 2)
                if p.tail:
                    po(tail, 3)
                nl(p, 0, 4)
                resid(p, 3)
                nl(p, 0, 5)
                if p.l1:
                    bn(p, x1, y_ok, yst, yst_ok, 1, 2, 3)
                    variance(p, yst, ymv, yvar, yst_ok, ymv_ok, yvar_ok, 1.0, 1e-5)
                if p.tail:
                    po_stats(tail, 3)
                hl(p, 0, 0)
                if p.l1:
                    resid_inv(p)
                    resid_norm(p, 0, 1)
                u(p, 0, 0)
                if p.setup:
                    weight(4)
                u(p, 0, 1)
                if p.tail:
                    fin(tail, 3)
                hl(p, 0, 1)
                if p.l1:
                    x1t(p)
                hl(p, 0, 2)
                hl(p, 0, 3)
                qk(p, 0, 1)
                if p.setup:
                    weight(5)
                qk(p, 2)
                den(p, 0, 0)
                den(p, 0, 1)
                if p.l0:
                    bn(p, z, z_ok[0], st, st_ok[0], 0, 1)
                    bn(p, z, z_ok[0], st, st_ok[0], 2, 3)
                    z_variance(p, 0)
                qk(p, 3, 4, 5)
                z_norm(p)
                norm_z(p, 0)
                if p.l1:
                    v(p, 0)
                norm_z(p, 1)
                scores(p, 0, 0)
                norm_z(p, 2, 3)
                scores(p, 0, 1)
                scores(p, 0, 2)
                if p.l1:
                    v(p, 1)
                scores(p, 0, 3)
                if p.l1:
                    v(p, 2)
                if p.l0:
                    th(p, 0)
                peaks(p, 0)
                if p.l0:
                    th(p, 1)
                    th(p, 2)
                if p.l1:
                    v(p, 3)
                if p.setup:
                    weight(6)
                pt(p, 0, 0, 1)
                scores(p, 1, 0)
                nl(p, 1, 0)
                pt(p, 0, 2)
                scores(p, 1, 1)
                pt(p, 0, 3)
                scores(p, 1, 2)
                guard(p, 0)
                scores(p, 1, 3)
                if p.l1:
                    pv(p, 0)
                nl(p, 1, 1)
                if p.setup:
                    weight(7)
                pt(p, 1, 0, 1)
                peaks(p, 1)
                nl(p, 1, 2, 3)
                if p.setup:
                    weight(8)
                pt(p, 1, 2, 3)
                if p.l1:
                    to(p, 0)
                scores(p, 2, 0)
                scores(p, 2, 1)
                nl(p, 1, 4)
                scores(p, 2, 2)
                scores(p, 2, 3)
                guard(p, 1)
                if p.l1:
                    po(p, 0)
                    pv(p, 1)
                peaks(p, 2)
                if p.l1:
                    po_stats(p, 0)
                nl(p, 1, 5)
                if p.setup:
                    weight(9)
                pt(p, 2, 0)
                if p.l1:
                    fin(p, 0)
                hl(p, 1, 0)
                pt(p, 2, 1, 2)
                if p.l1:
                    to(p, 1)
                pt(p, 2, 3)
                scores(p, 3, 0)
                scores(p, 3, 1)
                guard(p, 2)
                hl(p, 1, 1)
                scores(p, 3, 2)
                u(p, 1, 0)
                scores(p, 3, 3)
                if p.l1:
                    po(p, 1)
                peaks(p, 3)
                if p.l1:
                    pv(p, 2)
                    po_stats(p, 1)
                u(p, 1, 1)
                if p.l1:
                    to(p, 2)
                    fin(p, 1)
                pt(p, 3, 0, 1)
                guard(p, 3)
                pt(p, 3, 2)
                hl(p, 1, 2)
                hl(p, 1, 3)
                if p.nxt:
                    xt(p)
                pt(p, 3, 3)
                den(p, 1, 0)
                den(p, 1, 1)
                if p.l0:
                    bn(p, z, z_ok[1], st, st_ok[1], 0, 1)
                if p.l1:
                    po(p, 2)
                if p.l0:
                    bn(p, z, z_ok[1], st, st_ok[1], 2, 3)
                if p.l1:
                    po_stats(p, 2)

            def head():
                weight(0)
                weight(1)
                xt(prologue)

            passes(dve, body, head)

        @block.tensor
        def _(pe):
            def product(dst, terms, done, n=1, ready=None):
                total = len(terms)
                for i, (a, b) in enumerate(terms):
                    if ready and i % 3 == 0:
                        ready(i // 3)
                    last = mm(dst, a, b, start=(i == 0), stop=(i == total - 1))
                last.then_inc(done.sem, n)

            def half(n):
                return slice(64 * n, 64 * (n + 1))

            def split(a_hi, a_lo, b_hi, b_lo):
                return [(a_hi, b_hi), (a_hi, b_lo), (a_lo, b_hi)]

            def turn(stage, i, srcs, done):
                dst = bank(stage, i)
                for n, src in enumerate(srcs):
                    last = transpose(dst[:, n * 128:(n + 1) * 128], src, ident[:])
                last.then_inc(done.sem, 1)

            def xt(p):
                pe.wait_ge(x_in.sem, x_in.upto(p.it + 1, 16))
                for k in range(KB):
                    p.await_bank(pe, "xt", k)
                    turn("xt", k, [xin[:, b, k * 128:(k + 1) * 128] for b in range(GROUP)], xt_full)
                pe.wait_ge(adj_in.sem, adj_in.upto(p.it + 1, 16))
                p.await_bank(pe, "adjT", 0)
                turn("adjT", 0, [adjn[:, b] for b in range(GROUP)], adjT_full)

            def nl(p, l, *cs):
                def ready(k):
                    if l:
                        p.await_(pe, th_lo, k + 1)
                    else:
                        pe.wait_ge(xt_lo.sem, xt_lo.upto(p.it, k + 1))

                for c in cs if p.l0 else ():
                    lr, kb = divmod(c, KB)
                    if p.setup and kb == 0:
                        pe.wait_ge(w_lo_ok, 3 * l + lr + 1)
                    p.await_bank(pe, f"nl{l}", c)
                    w = slice(kb * 128, (kb + 1) * 128)
                    product(bank(f"nl{l}", c), [t for k in range(KB) for t in split(
                        wr_hi[:, 3 * l + lr, k, w], wr_lo[:, 3 * l + lr, k, w],
                        hT_hi[:, k].rearrange("p b t -> p (b t)"), hT_lo[:, k].rearrange("p b t -> p (b t)"))],
                        nl_full[l], ready=ready if c == 0 else None)

            def hl(p, l, *bs):
                for b in bs if p.l0 else ():
                    if p.setup and b == 0:
                        pe.wait_ge(w_lo_ok, 3 * l + 3)
                        pe.wait_ge(b_lo, 10)
                    p.await_bank(pe, f"hl{l}", b)
                    product(bank(f"hl{l}", b)[:, 0:FEAT], [t for k in range(KB) for t in split(
                        hT_hi[:, k, b], hT_lo[:, k, b], wr_hi[:, 3 * l + 2, k], wr_lo[:, 3 * l + 2, k])]
                        + [(ones_r[half(l)], bias_r[half(l)])], hl_full[l])

            def u(p, l, *hs):
                for h in hs if p.l0 else ():
                    if h == 0:
                        p.await_(pe, nl_lo[l], 2 * KB)
                    p.await_bank(pe, f"u{l}", h)
                    for g in range(2):
                        b = 2 * h + g
                        dst = bank(f"u{l}", h)[:, g * 256:(g + 1) * 256].rearrange("p (r t) -> p r t", r=2)
                        terms = [t for k in range(KB) for t in split(
                            hT_hi[:, k, b], hT_lo[:, k, b], nT_hi[:, k, :, b], nT_lo[:, k, :, b])]
                        for i, (a, m) in enumerate(terms):
                            last = mm(dst, a, m, start=(i == 0), stop=(i == len(terms) - 1))
                    last.then_inc(u_full[l].sem, 1)

            def ctx(p, l):
                if not p.l0:
                    return
                p.await_(pe, hlr_lo[l], GROUP)
                for b in range(GROUP):
                    if b % 2 == 0:
                        p.await_(pe, e_lo_ok[l], b // 2 + 1)
                    p.await_bank(pe, f"c{l}", b)
                    product(bank(f"c{l}", b)[:, 0:HCOL], split(e_hi[:, b], e_lo[:, b], hl_hi[:, b], hl_lo[:, b]),
                            c_full[l])

            def th(p, *ks):
                for k in ks if p.l0 else ():
                    if k == 0:
                        p.await_(pe, n_ok, GROUP)
                    p.await_bank(pe, "th", k)
                    turn("th", k, [z[:, b, k * 128:(k + 1) * 128] for b in range(GROUP)], th_full)

            def x1t(p):
                p.await_(pe, x1_ok, 2)
                p.await_(pe, x1_half, 2)
                for k in range(KB):
                    p.await_bank(pe, "x1t", k)
                    turn("x1t", k, [x1[:, b, k * 128:(k + 1) * 128] for b in range(GROUP)], x1t_full)

            def qk(p, *cs):
                for c in cs if p.l1 else ():
                    if c == 0 and not p.before.l1:
                        pe.wait_ge(w_lo_ok, 10)
                    p.await_bank(pe, "qk", c)
                    w = slice((c % KB) * 128, (c % KB + 1) * 128)
                    product(bank("qk", c), [t for k in range(KB) for t in split(
                        wh_hi[:, c // KB, k, w], wh_lo[:, c // KB, k, w],
                        xT_hi[:, k].rearrange("p b t -> p (b t)"), xT_lo[:, k].rearrange("p b t -> p (b t)"))],
                        qk_full, ready=(lambda k: p.await_(pe, x1t_lo, k + 1)) if c == 0 else None)

            def v(p, *bs):
                for b in bs if p.l1 else ():
                    p.await_bank(pe, "v", b)
                    product(bank("v", b)[:, 0:FEAT], [t for k in range(KB) for t in split(
                        xT_hi[:, k, b], xT_lo[:, k, b], wh_hi[:, 2, k], wh_lo[:, 2, k])]
                        + [(ones_h[half(0)], bias_h[half(0)])], v_full)

            def scores(p, b, *cs):
                if not p.l1:
                    return
                if 0 in cs and b == 0:
                    p.await_(pe, qkr_lo, 2 * KB)
                    if p.l0:
                        p.await_(pe, z_ok[0], GROUP)
                    elif p.before.l1:
                        p.before.await_(pe, s_ok, GROUP * TILES)
                elif 0 in cs:
                    p.await_(pe, s_ok, b * TILES)
                for c in cs:
                    for i in range(3):
                        a, m = ((qk_hi, qk_hi), (qk_hi, qk_lo), (qk_lo, qk_hi))[i]
                        for j in range(TILES):
                            rows = slice(HEAD * j, HEAD * (j + 1))
                            last = mm(psum[:, SC[j], c * TOK:(c + 1) * TOK], a[rows, 0, c, b], m[rows, 1, c, b],
                                      start=(i == 0), stop=(i == 2))
                            if c == KB - 1 and i == 2:
                                last.then_inc(s_full.sem, 1)

            def pt(p, b, *js):
                for j in js if p.l1 else ():
                    n = b * TILES + j
                    p.await_bank(pe, "pt", n)
                    p.await_(pe, p_ok, n + 1)
                    turn("pt", n, [w[:, TILES * c + j] for c in range(KB)], pt_full)

            def pv(run, b):
                p = run.earlier() if b == 3 else run
                p.await_(pe, vr_lo, b + 1)
                if b == 3:
                    run.await_bank(pe, "pv", b)
                p.await_(pe, pt_lo, (b + 1) * TILES)
                dst = bank("pv", b)
                for h in range(HEADS):
                    terms = split(pT_hi[:, h], pT_lo[:, h], v_hi[:, b, h], v_lo[:, b, h])
                    for i, (a, m) in enumerate(terms):
                        last = mm(dst[:, h * VCOL:(h + 1) * VCOL], a, m, start=(i == 0), stop=(i == 2))
                last.then_inc(pv_full.sem, 1)

            def to(run, b):
                p = run.earlier() if b == 3 else run
                p.await_(pe, o_ok, b + 1)
                run.await_bank(pe, "to", b)
                of = o[:].rearrange("p h d -> p (h d)")
                turn("to", b, [of[:, k * 128:(k + 1) * 128] for k in range(KB)], to_full)

            def po(run, b):
                p = run.earlier() if b == 3 else run
                p.await_(pe, to_lo, b + 1)
                run.await_bank(pe, "po", b)
                product(bank("po", b)[:, 0:FEAT], [t for k in range(KB) for t in split(
                    oT_hi[:, k], oT_lo[:, k], wh_hi[:, 3, k], wh_lo[:, 3, k])]
                    + [(ones_h[half(1)], bias_h[half(1)])], po_full)

            def body(p):
                nl(p, 0, 0)
                if p.tail:
                    pv(p, 3)
                nl(p, 0, 1, 2)
                if p.tail:
                    to(p, 3)
                nl(p, 0, 3, 4)
                if p.tail:
                    po(p, 3)
                nl(p, 0, 5)
                hl(p, 0, 0, 1)
                u(p, 0, 0, 1)
                if p.l1:
                    x1t(p)
                hl(p, 0, 2, 3)
                qk(p, 0, 1, 2)
                ctx(p, 0)
                qk(p, 3, 4, 5)
                v(p, 0)
                scores(p, 0, 0, 1, 2)
                v(p, 1, 2)
                th(p, 0, 1)
                v(p, 3)
                th(p, 2)
                scores(p, 1, 0)
                pt(p, 0, 0)
                scores(p, 1, 1, 2)
                nl(p, 1, 0)
                pt(p, 0, 1, 2, 3)
                nl(p, 1, 1)
                if p.l1:
                    pv(p, 0)
                nl(p, 1, 2)
                pt(p, 1, 0, 1)
                nl(p, 1, 3)
                scores(p, 2, 0)
                pt(p, 1, 2)
                scores(p, 2, 1)
                pt(p, 1, 3)
                scores(p, 2, 2)
                if p.l1:
                    to(p, 0)
                nl(p, 1, 4)
                if p.l1:
                    pv(p, 1)
                    po(p, 0)
                nl(p, 1, 5)
                pt(p, 2, 0, 1)
                hl(p, 1, 0)
                scores(p, 3, 0)
                pt(p, 2, 2)
                scores(p, 3, 1, 2)
                if p.l1:
                    to(p, 1)
                pt(p, 2, 3)
                hl(p, 1, 1)
                if p.l1:
                    po(p, 1)
                u(p, 1, 0)
                if p.l1:
                    pv(p, 2)
                u(p, 1, 1)
                pt(p, 3, 0)
                if p.l1:
                    to(p, 2)
                pt(p, 3, 1)
                hl(p, 1, 2)
                pt(p, 3, 2)
                hl(p, 1, 3)
                pt(p, 3, 3)
                if p.nxt:
                    xt(p)
                ctx(p, 1)
                if p.l1:
                    po(p, 2)

            def head():
                pe.wait_ge(const_ok, 4)
                xt(prologue)
                pe.wait_ge(ones_ok, 9)

            passes(pe, body, head)


def kernel(x, adj, L0_gnn_W_left, L0_gnn_W_right, L0_gnn_W_lin, L0_gnn_b_lin, L0_gnn_ln_a, L0_gnn_ln_b,
           L1_gnn_Wq, L1_gnn_Wk, L1_gnn_Wv, L1_gnn_bv, L1_gnn_Wo, L1_gnn_bo):
    import numpy as np
    import concourse.bacc as bacc
    from concourse.bass_utils import run_bass_kernel_spmd

    def rows(w):
        return np.asarray(w).reshape(KB, 128, FEAT).transpose(1, 0, 2)

    per_layer = [(L0_gnn_W_left[l], L0_gnn_W_right[l], np.asarray(L0_gnn_W_lin[l]).T) for l in range(2)]
    l1 = [np.asarray(w).T for w in (L1_gnn_Wq, L1_gnn_Wk, L1_gnn_Wv, L1_gnn_Wo)]
    a, b = np.asarray(L0_gnn_ln_a), np.asarray(L0_gnn_ln_b)
    arrays = {
        "x": np.asarray(x),
        "adj": np.asarray(adj),
        "weights": np.stack([rows(w) for w in (*per_layer[0], *per_layer[1], *l1)]),
        "biases": np.stack([np.asarray(v) for v in (L0_gnn_b_lin[0], L0_gnn_b_lin[1], L1_gnn_bv, L1_gnn_bo)]),
        "ln_cols": np.ascontiguousarray(np.stack([a[0].reshape(KB, 128), b[0].reshape(KB, 128)]).transpose(2, 0, 1)),
        "ln_rows": np.stack([a[1], b[1]]),
    }
    nc = bacc.Bacc("TRN2", target_bir_lowering=False, num_devices=1, dynamic_dma_scratch_size=1024)
    args = [nc.dram_tensor(n, v.shape, mybir.dt.from_np(v.dtype), kind="ExternalInput").ap()
            for n, v in arrays.items()]
    out = nc.dram_tensor("out", (GRAPHS, TOK, FEAT), mybir.dt.float32, kind="ExternalOutput").ap()
    program(nc, *args, out)
    return run_bass_kernel_spmd(nc, [arrays], core_ids=[0]).results[0]["out"]
```
